# Optimizing a Trainium2 kernel written in Bass

```python
import numpy as np
import jax
import jax.numpy as jnp

def _softmax(x, axis=-1):
    return jax.nn.softmax(x, axis=axis)

def _gelu(x):
    return jax.nn.gelu(x, approximate=True)

def _silu(x):
    return jax.nn.silu(x)

def _sigmoid(x):
    return jax.nn.sigmoid(x)

def _layernorm(x, axis=-1, eps=1e-05):
    m = jnp.mean(x, axis=axis, keepdims=True)
    v = jnp.var(x, axis=axis, keepdims=True)
    return (x - m) / jnp.sqrt(v + eps)

def _scatter_add(tgt, idx, src, axis=0):
    return tgt.at[idx].add(src)

def _segment_sum(src, seg, n):
    return jax.ops.segment_sum(src, seg, n)
kernel_name = 'mk_dlrm_tower_d1_rec_r8_172a84'

def setup_inputs(seed: int=0):
    np.random.seed(seed)
    _w = jnp.asarray

    def _rec_inputs():
        import jax
        import jax.numpy as jnp
        _tk = jax.random.key(seed)
        dense_ctx = jax.random.normal(jax.random.fold_in(_tk, 190), (512, 16), jnp.float32)
        ids = jnp.stack([jax.random.randint(jax.random.fold_in(_tk, 200 + f), (512,), 0, v, jnp.int32) for f, v in enumerate([12500, 1000, 1250, 1000, 125000, 12500, 1250, 1000, 1000, 12500, 12500, 125000, 12500, 1000, 12500, 1250, 125000, 1000, 1000, 1250, 125000, 12500, 125000, 1250, 12500, 12500, 125000, 125000, 125000, 1250, 12500, 1250, 1000, 1250, 1250, 12500, 12500, 12500, 1250])], axis=1)
        tbl_0 = 0.05 * jax.random.normal(jax.random.fold_in(_tk, 500 + 0), (12500, 16), jnp.float32)
        tbl_1 = 0.05 * jax.random.normal(jax.random.fold_in(_tk, 500 + 1), (1000, 16), jnp.float32)
        tbl_2 = 0.05 * jax.random.normal(jax.random.fold_in(_tk, 500 + 2), (1250, 16), jnp.float32)
        tbl_3 = 0.05 * jax.random.normal(jax.random.fold_in(_tk, 500 + 3), (1000, 16), jnp.float32)
        tbl_4 = 0.05 * jax.random.normal(jax.random.fold_in(_tk, 500 + 4), (125000, 16), jnp.float32)
        tbl_5 = 0.05 * jax.random.normal(jax.random.fold_in(_tk, 500 + 5), (12500, 16), jnp.float32)
        tbl_6 = 0.05 * jax.random.normal(jax.random.fold_in(_tk, 500 + 6), (1250, 16), jnp.float32)
        tbl_7 = 0.05 * jax.random.normal(jax.random.fold_in(_tk, 500 + 7), (1000, 16), jnp.float32)
        tbl_8 = 0.05 * jax.random.normal(jax.random.fold_in(_tk, 500 + 8), (1000, 16), jnp.float32)
        tbl_9 = 0.05 * jax.random.normal(jax.random.fold_in(_tk, 500 + 9), (12500, 16), jnp.float32)
        tbl_10 = 0.05 * jax.random.normal(jax.random.fold_in(_tk, 500 + 10), (12500, 16), jnp.float32)
        tbl_11 = 0.05 * jax.random.normal(jax.random.fold_in(_tk, 500 + 11), (125000, 16), jnp.float32)
        tbl_12 = 0.05 * jax.random.normal(jax.random.fold_in(_tk, 500 + 12), (12500, 16), jnp.float32)
        tbl_13 = 0.05 * jax.random.normal(jax.random.fold_in(_tk, 500 + 13), (1000, 16), jnp.float32)
        tbl_14 = 0.05 * jax.random.normal(jax.random.fold_in(_tk, 500 + 14), (12500, 16), jnp.float32)
        tbl_15 = 0.05 * jax.random.normal(jax.random.fold_in(_tk, 500 + 15), (1250, 16), jnp.float32)
        tbl_16 = 0.05 * jax.random.normal(jax.random.fold_in(_tk, 500 + 16), (125000, 16), jnp.float32)
        tbl_17 = 0.05 * jax.random.normal(jax.random.fold_in(_tk, 500 + 17), (1000, 16), jnp.float32)
        tbl_18 = 0.05 * jax.random.normal(jax.random.fold_in(_tk, 500 + 18), (1000, 16), jnp.float32)
        tbl_19 = 0.05 * jax.random.normal(jax.random.fold_in(_tk, 500 + 19), (1250, 16), jnp.float32)
        tbl_20 = 0.05 * jax.random.normal(jax.random.fold_in(_tk, 500 + 20), (125000, 16), jnp.float32)
        tbl_21 = 0.05 * jax.random.normal(jax.random.fold_in(_tk, 500 + 21), (12500, 16), jnp.float32)
        tbl_22 = 0.05 * jax.random.normal(jax.random.fold_in(_tk, 500 + 22), (125000, 16), jnp.float32)
        tbl_23 = 0.05 * jax.random.normal(jax.random.fold_in(_tk, 500 + 23), (1250, 16), jnp.float32)
        tbl_24 = 0.05 * jax.random.normal(jax.random.fold_in(_tk, 500 + 24), (12500, 16), jnp.float32)
        tbl_25 = 0.05 * jax.random.normal(jax.random.fold_in(_tk, 500 + 25), (12500, 16), jnp.float32)
        tbl_26 = 0.05 * jax.random.normal(jax.random.fold_in(_tk, 500 + 26), (125000, 16), jnp.float32)
        tbl_27 = 0.05 * jax.random.normal(jax.random.fold_in(_tk, 500 + 27), (125000, 16), jnp.float32)
        tbl_28 = 0.05 * jax.random.normal(jax.random.fold_in(_tk, 500 + 28), (125000, 16), jnp.float32)
        tbl_29 = 0.05 * jax.random.normal(jax.random.fold_in(_tk, 500 + 29), (1250, 16), jnp.float32)
        tbl_30 = 0.05 * jax.random.normal(jax.random.fold_in(_tk, 500 + 30), (12500, 16), jnp.float32)
        tbl_31 = 0.05 * jax.random.normal(jax.random.fold_in(_tk, 500 + 31), (1250, 16), jnp.float32)
        tbl_32 = 0.05 * jax.random.normal(jax.random.fold_in(_tk, 500 + 32), (1000, 16), jnp.float32)
        tbl_33 = 0.05 * jax.random.normal(jax.random.fold_in(_tk, 500 + 33), (1250, 16), jnp.float32)
        tbl_34 = 0.05 * jax.random.normal(jax.random.fold_in(_tk, 500 + 34), (1250, 16), jnp.float32)
        tbl_35 = 0.05 * jax.random.normal(jax.random.fold_in(_tk, 500 + 35), (12500, 16), jnp.float32)
        tbl_36 = 0.05 * jax.random.normal(jax.random.fold_in(_tk, 500 + 36), (12500, 16), jnp.float32)
        tbl_37 = 0.05 * jax.random.normal(jax.random.fold_in(_tk, 500 + 37), (12500, 16), jnp.float32)
        tbl_38 = 0.05 * jax.random.normal(jax.random.fold_in(_tk, 500 + 38), (1250, 16), jnp.float32)
        _rk = jax.random.fold_in(_tk, 7)
        W_top1 = 0.0606339 * jax.random.normal(jax.random.fold_in(_tk, 801), (272, 512), jnp.float32)
        W_top2 = 0.0441942 * jax.random.normal(jax.random.fold_in(_tk, 802), (512, 256), jnp.float32)
        W_top3 = 0.0625 * jax.random.normal(jax.random.fold_in(_tk, 803), (256, 1), jnp.float32)
        b_top1 = jnp.zeros((512,), jnp.float32)
        b_top2 = jnp.zeros((256,), jnp.float32)
        return (dense_ctx, ids, tbl_0, tbl_1, tbl_2, tbl_3, tbl_4, tbl_5, tbl_6, tbl_7, tbl_8, tbl_9, tbl_10, tbl_11, tbl_12, tbl_13, tbl_14, tbl_15, tbl_16, tbl_17, tbl_18, tbl_19, tbl_20, tbl_21, tbl_22, tbl_23, tbl_24, tbl_25, tbl_26, tbl_27, tbl_28, tbl_29, tbl_30, tbl_31, tbl_32, tbl_33, tbl_34, tbl_35, tbl_36, tbl_37, tbl_38, W_top1, b_top1, W_top2, b_top2, W_top3)
    dense_ctx, ids, tbl_0, tbl_1, tbl_2, tbl_3, tbl_4, tbl_5, tbl_6, tbl_7, tbl_8, tbl_9, tbl_10, tbl_11, tbl_12, tbl_13, tbl_14, tbl_15, tbl_16, tbl_17, tbl_18, tbl_19, tbl_20, tbl_21, tbl_22, tbl_23, tbl_24, tbl_25, tbl_26, tbl_27, tbl_28, tbl_29, tbl_30, tbl_31, tbl_32, tbl_33, tbl_34, tbl_35, tbl_36, tbl_37, tbl_38, W_top1, b_top1, W_top2, b_top2, W_top3 = _rec_inputs()

    def _L0_rec_setup():
        import jax, jax.numpy as jnp
        import numpy as np
        B, M, D = (1024, 39, 16)
        S1, S2 = (128, 128)

        def _cin_layer(x0, xk, W, b):
            out = jnp.einsum('bhd,bmd,shm->bsd', xk, x0, W) + b[None, :, None]
            return jax.nn.relu(out)
        key = jax.random.key(seed)
        k0, k1, k2 = jax.random.split(key, 3)
        x0 = jax.random.normal(k0, (B, M, D), dtype=jnp.float32)
        W1 = jax.random.normal(k1, (S1, M, M), dtype=jnp.float32) * 0.05
        b1 = jnp.zeros((S1,), dtype=jnp.float32)
        W2 = jax.random.normal(k2, (S2, S1, M), dtype=jnp.float32) * 0.05
        b2 = jnp.zeros((S2,), dtype=jnp.float32)
        return {'x0': x0, 'W1': W1, 'b1': b1, 'W2': W2, 'b2': b2}
    _L0_rec_all = _L0_rec_setup()
    _L0_rec_in = {k: v for k, v in _L0_rec_all.items() if k in ('W1', 'b1', 'W2', 'b2')}
    del _L0_rec_all
    return {'dense_ctx': dense_ctx, 'ids': ids, 'tbl_0': tbl_0, 'tbl_1': tbl_1, 'tbl_2': tbl_2, 'tbl_3': tbl_3, 'tbl_4': tbl_4, 'tbl_5': tbl_5, 'tbl_6': tbl_6, 'tbl_7': tbl_7, 'tbl_8': tbl_8, 'tbl_9': tbl_9, 'tbl_10': tbl_10, 'tbl_11': tbl_11, 'tbl_12': tbl_12, 'tbl_13': tbl_13, 'tbl_14': tbl_14, 'tbl_15': tbl_15, 'tbl_16': tbl_16, 'tbl_17': tbl_17, 'tbl_18': tbl_18, 'tbl_19': tbl_19, 'tbl_20': tbl_20, 'tbl_21': tbl_21, 'tbl_22': tbl_22, 'tbl_23': tbl_23, 'tbl_24': tbl_24, 'tbl_25': tbl_25, 'tbl_26': tbl_26, 'tbl_27': tbl_27, 'tbl_28': tbl_28, 'tbl_29': tbl_29, 'tbl_30': tbl_30, 'tbl_31': tbl_31, 'tbl_32': tbl_32, 'tbl_33': tbl_33, 'tbl_34': tbl_34, 'tbl_35': tbl_35, 'tbl_36': tbl_36, 'tbl_37': tbl_37, 'tbl_38': tbl_38, 'W_top1': W_top1, 'b_top1': b_top1, 'W_top2': W_top2, 'b_top2': b_top2, 'W_top3': W_top3, 'L0_rec_W1': _L0_rec_in['W1'], 'L0_rec_b1': _L0_rec_in['b1'], 'L0_rec_W2': _L0_rec_in['W2'], 'L0_rec_b2': _L0_rec_in['b2']}

def reference(dense_ctx, ids, tbl_0, tbl_1, tbl_2, tbl_3, tbl_4, tbl_5, tbl_6, tbl_7, tbl_8, tbl_9, tbl_10, tbl_11, tbl_12, tbl_13, tbl_14, tbl_15, tbl_16, tbl_17, tbl_18, tbl_19, tbl_20, tbl_21, tbl_22, tbl_23, tbl_24, tbl_25, tbl_26, tbl_27, tbl_28, tbl_29, tbl_30, tbl_31, tbl_32, tbl_33, tbl_34, tbl_35, tbl_36, tbl_37, tbl_38, W_top1, b_top1, W_top2, b_top2, W_top3, L0_rec_W1, L0_rec_b1, L0_rec_W2, L0_rec_b2):
    import jax
    import jax.numpy as jnp

    def _L0_rec_ref(x0, W1, b1, W2, b2):
        import jax, jax.numpy as jnp
        import numpy as np
        B, M, D = (1024, 39, 16)
        S1, S2 = (128, 128)

        def _cin_layer(x0, xk, W, b):
            out = jnp.einsum('bhd,bmd,shm->bsd', xk, x0, W) + b[None, :, None]
            return jax.nn.relu(out)
        x1 = _cin_layer(x0, x0, W1, b1)
        x2 = _cin_layer(x0, x1, W2, b2)
        p1 = x1.sum(axis=-1)
        p2 = x2.sum(axis=-1)
        return jnp.concatenate([p1, p2], axis=-1)
    e = jnp.stack([tbl_0[ids[:, 0]], tbl_1[ids[:, 1]], tbl_2[ids[:, 2]], tbl_3[ids[:, 3]], tbl_4[ids[:, 4]], tbl_5[ids[:, 5]], tbl_6[ids[:, 6]], tbl_7[ids[:, 7]], tbl_8[ids[:, 8]], tbl_9[ids[:, 9]], tbl_10[ids[:, 10]], tbl_11[ids[:, 11]], tbl_12[ids[:, 12]], tbl_13[ids[:, 13]], tbl_14[ids[:, 14]], tbl_15[ids[:, 15]], tbl_16[ids[:, 16]], tbl_17[ids[:, 17]], tbl_18[ids[:, 18]], tbl_19[ids[:, 19]], tbl_20[ids[:, 20]], tbl_21[ids[:, 21]], tbl_22[ids[:, 22]], tbl_23[ids[:, 23]], tbl_24[ids[:, 24]], tbl_25[ids[:, 25]], tbl_26[ids[:, 26]], tbl_27[ids[:, 27]], tbl_28[ids[:, 28]], tbl_29[ids[:, 29]], tbl_30[ids[:, 30]], tbl_31[ids[:, 31]], tbl_32[ids[:, 32]], tbl_33[ids[:, 33]], tbl_34[ids[:, 34]], tbl_35[ids[:, 35]], tbl_36[ids[:, 36]], tbl_37[ids[:, 37]], tbl_38[ids[:, 38]]], axis=1)
    z = _L0_rec_ref(e, L0_rec_W1, L0_rec_b1, L0_rec_W2, L0_rec_b2)
    z = z.reshape(z.shape[0], -1)
    h = jnp.concatenate([z, dense_ctx], axis=1)
    h = jnp.maximum(h @ W_top1 + b_top1, 0.0)
    h = jnp.maximum(h @ W_top2 + b_top2, 0.0)
    y = h @ W_top3
    return y

_drawn_inputs = setup_inputs


def setup_inputs(seed=0):
    import zlib

    import numpy as np

    out = dict(_drawn_inputs(seed))
    spreads = {'b_top1': (0.0, 0.1),
     'b_top2': (0.0, 0.1),
     'L0_rec_b1': (0.0, 0.1),
     'L0_rec_b2': (0.0, 0.1)}
    factors = {'tbl_0': 4.808,
     'tbl_1': 4.338,
     'tbl_2': 7.198,
     'tbl_3': 5.82,
     'tbl_4': 6.849,
     'tbl_5': 7.147,
     'tbl_6': 6.168,
     'tbl_7': 4.921,
     'tbl_8': 8.0,
     'tbl_9': 7.84,
     'tbl_10': 6.794,
     'tbl_11': 5.881,
     'tbl_12': 5.472,
     'tbl_14': 8.0,
     'tbl_15': 6.928,
     'tbl_16': 7.414,
     'tbl_17': 4.991,
     'tbl_18': 5.935,
     'tbl_19': 4.543,
     'tbl_20': 8.0,
     'tbl_21': 3.555,
     'tbl_22': 8.0,
     'tbl_23': 7.924,
     'tbl_24': 7.381,
     'tbl_25': 5.171,
     'tbl_26': 4.6,
     'tbl_27': 6.284,
     'tbl_28': 8.0,
     'tbl_29': 5.508,
     'tbl_30': 5.17,
     'tbl_31': 3.119,
     'tbl_32': 8.0,
     'tbl_33': 8.0,
     'tbl_34': 7.433,
     'tbl_35': 7.032,
     'tbl_36': 8.0,
     'tbl_37': 8.0,
     'tbl_38': 6.123,
     'tbl_13': 3.968}
    for name, (base, spread) in spreads.items():
        noise = np.random.default_rng([zlib.crc32(name.encode()), seed]).standard_normal(out[name].shape)
        drawn = base * np.exp(spread * noise) if base else spread * noise
        out[name] = jnp.asarray(drawn.astype(out[name].dtype))
    for name, factor in factors.items():
        out[name] = (out[name] * factor).astype(out[name].dtype)
    return out
```

```python
from contextlib import ExitStack

import concourse.bass as bass
from concourse import mybir

ALU = mybir.AluOpType
ACT = mybir.ActivationFunctionType
AX_X = mybir.AxisListType.X
F32 = mybir.dt.float32
I32 = mybir.dt.int32

P = 128
B, M, D = 512, 39, 16
S = 128
TILES = B // P
QN = 4
DH = 2
DQ = D // QN
QH = QN // DH
N = DQ * P
CHUNKS = TILES * QN

SHIFTS = (M + 1) // 2
KG = P // M
L1_ROWS = KG * M
L1_TILES = -(-SHIFTS // KG)
L1_LAST = (SHIFTS - KG * (L1_TILES - 1)) * M
X_ROWS = M + SHIFTS

MG = 4
HG = P // MG
J = M // MG
I = S // HG
SINGLE = M - MG * J
L2_TILES = I * J + SINGLE
XB = J + SINGLE
G3 = 3
GROUPS = L2_TILES // G3
RING = 4

H1, H2 = 512, 256
O1, O2 = H1 // P, H2 // P
DENSE = 16
SMALL = 6 + 2 * O2 + O1


def in_register(engine, value):
    return value if isinstance(value, int) else engine.snap(value)


def build(nc, dense_ctx, ids, tables, W_top1, b_top1, W_top2, b_top2, W_top3, W1, b1, W2, b2, out):
    assert J % G3 == 0 and SINGLE == G3 and L2_TILES % G3 == 0 and (GROUPS * QN) % RING == 0

    with ExitStack() as ctx:
        def sb(name, shape, dt=F32):
            return ctx.enter_context(nc.sbuf_tensor(name, shape, dt))

        def ps(name, shape):
            return ctx.enter_context(nc.psum_tensor(name, shape, F32))

        def sem(name):
            return ctx.enter_context(nc.semaphore(name))

        x_scratch = nc.dram_tensor("x_scratch", [CHUNKS, X_ROWS, N], F32)
        x1_scratch = nc.dram_tensor("x1_scratch", [2, S, N], F32)

        ident = sb("ident", [P, P])
        ids_sb = sb("ids_sb", [P, TILES, M], I32)
        dense_sb = sb("dense_sb", [P, TILES, DENSE])
        denseT = sb("denseT", [DENSE, TILES * P])
        emb = sb("emb", [P, M, D])
        xT = sb("xT", [DH * M, QN // DH, N])
        w1T = sb("w1T", [P, L1_TILES, S])
        w2T = sb("w2T", [P, L2_TILES, S])
        b1_sb = sb("b1_sb", [S, 1])
        b2_sb = sb("b2_sb", [S, 1])
        wt1a = sb("wt1a", [P, 2, H1])
        wt1b = sb("wt1b", [DENSE, H1])
        wt2 = sb("wt2", [P, O1, H2])
        wt3 = sb("wt3", [P, O2, 1])
        bt1 = sb("bt1", [P, O1])
        bt2 = sb("bt2", [P, O2])

        l1_a = sb("l1_a", [P, 2, N])
        l1_b = sb("l1_b", [P, 2, L1_TILES, N])
        x0_rep = sb("x0_rep", [P, 2, XB, N])
        x1_rep = sb("x1_rep", [P, 2, I, N])
        prod1 = sb("prod1", [P, L1_TILES, N])
        prod2 = sb("prod2", [P, RING, G3, N])
        x1 = sb("x1", [S, QN, DQ, P])
        x2 = sb("x2", [S, QN, DQ, P])
        p1 = sb("p1", [S, P])
        p2 = sb("p2", [S, P])
        h1 = sb("h1", [P, O1, P])
        h2 = sb("h2", [P, O2, P])
        y_sb = sb("y_sb", [1, P])
        x0_rep1 = x0_rep[:, 1, :, :].rearrange("p a n -> p (a n)")
        w2_raw = x0_rep1[:, 0:S * M].rearrange("p (h m) -> p h m", m=M)
        w1_sym = x0_rep1[:, S * M:S * M + SHIFTS * M]
        w2_packed = prod2[:, :, :, :].rearrange("p a c n -> p (a c n)")[:, 0:I * J * P]
        w1_raw = x1_rep[:, 1, :, :].rearrange("p a n -> p (a n)")[:, 0:M * M]

        x1_ps = [ps(f"x1_ps{i}", [P, N]) for i in range(2)]
        x2_ps = [ps(f"x2_ps{i}", [P, N]) for i in range(2)]
        tr_ps = [ps(f"tr_ps{i}", [P, N]) for i in range(2)]
        h_ps = ps("h_ps", [P, N])
        y_ps = ps("y_ps", [P, N])

        ids_in = sem("ids_in")
        w1_in = sem("w1_in")
        w2_in = sem("w2_in")
        small_in = sem("small_in")
        ident_zero = sem("ident_zero")
        ident_ready = sem("ident_ready")
        gathered = sem("gathered")
        w1_symmetric = sem("w1_symmetric")
        w2_packed_act = sem("w2_packed_act")
        w2_packed_dve = sem("w2_packed_dve")
        w_turned = sem("w_turned")
        w_copied_act = sem("w_copied_act")
        w_copied_dve = sem("w_copied_dve")
        x_turned = sem("x_turned")
        x_copied = sem("x_copied")
        x_scratched = sem("x_scratched")
        l1_in = [sem(f"l1_in{i}") for i in range(2)]
        x0_rep_in = [sem(f"x0_rep_in{i}") for i in range(2)]
        x1_rep_in = [sem(f"x1_rep_in{i}") for i in range(2)]
        prod1_ready = sem("prod1_ready")
        l1_done = sem("l1_done")
        x1_ready = sem("x1_ready")
        x1_scratched = sem("x1_scratched")
        prod2_ready = sem("prod2_ready")
        l2_done = sem("l2_done")
        x2_ready = sem("x2_ready")
        p1_ready = sem("p1_ready")
        p2_ready = sem("p2_ready")
        h1_summed = sem("h1_summed")
        h1_ready = sem("h1_ready")
        h2_summed = sem("h2_summed")
        h2_ready = sem("h2_ready")
        y_summed = sem("y_summed")
        y_ready = sem("y_ready")
        y_out = sem("y_out")

        def w_banks():
            singles = [(w1T[0:(L1_ROWS if j < L1_TILES - 1 else L1_LAST), j, :],
                        w1_sym[:, j * L1_ROWS:min((j + 1) * L1_ROWS, SHIFTS * M)]) for j in range(L1_TILES)]
            for i in range(I):
                for j in range(J):
                    n = i * J + j
                    singles.append((w2T[:, n, :], w2_packed[:, n * P:(n + 1) * P]))
            for k in range(SINGLE):
                singles.append((w2T[:, I * J + k, :], w2_raw[:, :, J * MG + k]))
            return singles

        turns = w_banks()
        banks = [turns[0:4], turns[4:L1_TILES - 1], turns[L1_TILES - 1:L1_TILES]]
        banks += [turns[k:k + 4] for k in range(L1_TILES, len(turns), 4)]
        heights = [L1_ROWS, L1_ROWS, L1_LAST] + [P] * (len(banks) - 3)
        firsts = [0, 4, L1_TILES - 1] + [k for k in range(0, L2_TILES, 4)]

        def pack_w2(engine_copy, i):
            return engine_copy(w2_packed[:, i * J * P:(i + 1) * J * P].rearrange("s (a h) -> s a h", h=HG),
                               w2_raw[:, i * HG:(i + 1) * HG, 0:J * MG].rearrange("s h a -> s a h"))

        def bank_dst(n):
            w = w1T if n < 3 else w2T
            return w[0:heights[n], firsts[n]:firsts[n] + len(banks[n]), :]

        def bank_src(n):
            return tr_ps[n % 2][0:heights[n], 0:len(banks[n]) * S].rearrange("p (k s) -> p k s", s=S)

        BANKS = len(banks) + 1

        block = ctx.enter_context(nc.Block())

        @block.sync
        def _(sp):
            sp.dma_start(ids_sb[:], ids.rearrange("(t p) f -> p t f", p=P)).then_inc(ids_in, 16)
            sp.dma_start(w1_raw, W1.rearrange("s h m -> s (h m)")).then_inc(w1_in, 16)
            sp.dma_start(w2_raw, W2).then_inc(w2_in, 16)
            sp.dma_start(dense_sb[:], dense_ctx.rearrange("(t p) c -> p t c", p=P)).then_inc(small_in, 16)
            sp.dma_start(b1_sb[:], b1.rearrange("(s a) -> s a", a=1)).then_inc(small_in, 16)
            sp.dma_start(b2_sb[:], b2.rearrange("(s a) -> s a", a=1)).then_inc(small_in, 16)
            sp.dma_start(wt1a[:], W_top1[0:2 * P, :].rearrange("(k p) n -> p k n", p=P)).then_inc(small_in, 16)
            sp.dma_start(wt1b[:], W_top1[2 * P:2 * P + DENSE, :]).then_inc(small_in, 16)
            sp.dma_start(wt2[:], W_top2.rearrange("(k p) n -> p k n", p=P)).then_inc(small_in, 16)
            for vector, columns in ((W_top3.rearrange("k a -> (k a)"), wt3[:, :, 0]), (b_top1, bt1), (b_top2, bt2)):
                for k in range(vector.shape[0] // P):
                    sp.dma_start(columns[:, k:k + 1], vector[k * P:(k + 1) * P].rearrange("(p a) -> p a", a=1)
                                 ).then_inc(small_in, 16)

            def store_x(t):
                at = [in_register(sp, (QN * t * X_ROWS + r0) * N) for r0 in (0, M)]
                sp.wait_ge(x_copied, QH * (t + 1))
                for base, rows in zip(at, (M, SHIFTS)):
                    for k in range(QH):
                        dst = bass.AP(x_scratch, base + k * X_ROWS * N, [[N, rows], [QH * X_ROWS * N, DH], [1, N]])
                        sp.dma_start(dst, xT[0:DH * rows, k, :]).then_inc(x_scratched, 16)

            def load_l1(t, q):
                g, par = QN * t + q, q % 2
                base = in_register(sp, g * X_ROWS * N)
                sp.wait_ge(x_scratched, 16 * 2 * QH * (t + 1))
                sp.dma_start(l1_a[0:L1_ROWS, par, :],
                             bass.AP(x_scratch, base, [[0, KG], [N, M], [1, N]])).then_inc(l1_in[par], 16)
                for j in range(L1_TILES):
                    ks = KG if j < L1_TILES - 1 else SHIFTS - KG * (L1_TILES - 1)
                    sp.dma_start(l1_b[0:ks * M, par, j, :],
                                 bass.AP(x_scratch, base + KG * j * N, [[N, ks], [N, M], [1, N]])
                                 ).then_inc(l1_in[par], 16)

            def load_x0_rep(t, q, uses=None):
                g, par = QN * t + q, q % 2
                base = in_register(sp, g * X_ROWS * N)
                if uses is not None:
                    sp.wait_ge(prod2_ready, uses)
                for j in range(J):
                    sp.dma_start(x0_rep[:, par, j, :],
                                 bass.AP(x_scratch, base + MG * j * N, [[N, MG], [0, HG], [1, N]])
                                 ).then_inc(x0_rep_in[par], 16)
                sp.dma_start(x0_rep[:, par, J:XB, :],
                             bass.AP(x_scratch, base + MG * J * N, [[0, P], [N, SINGLE], [1, N]])
                             ).then_inc(x0_rep_in[par], 16)

            def repeat_x1(t, q):
                g, par = QN * t + q, q % 2
                sp.wait_ge(x1_ready, g + 1)
                sp.dma_start(x1_scratch[par], x1[:, q, :, :].rearrange("s d b -> s (d b)")).then_inc(x1_scratched, 16)
                sp.wait_ge(x1_scratched, 16 * (g + 1))
                for i in range(I):
                    sp.dma_start(x1_rep[:, par, i, :],
                                 bass.AP(x1_scratch, (par * S + i * HG) * N, [[0, MG], [N, HG], [1, N]])
                                 ).then_inc(x1_rep_in[par], 16)

            def step(t, q, ahead=True, ahead2=True):
                g = QN * t + q
                if ahead:
                    t1, q1 = (t, q + 1) if q + 1 < QN else (t + 1, 0)
                    load_x0_rep(t1, q1, None if isinstance(g, int) and g == 0 else GROUPS * g)
                    repeat_x1(t1, q1)
                if ahead2:
                    t2, q2 = (t, q + 2) if q + 2 < QN else (t + 1, q + 2 - QN)
                    load_l1(t2, q2)

            def store_y(t):
                at = in_register(sp, P * t)
                sp.wait_ge(y_ready, t + 1)
                sp.dma_start(bass.AP(out.tensor, at, [[P, 1], [1, P]]), y_sb[:]).then_inc(y_out, 16)

            store_x(0)
            load_l1(0, 0)
            load_x0_rep(0, 0)
            load_l1(0, 1)
            repeat_x1(0, 0)
            sp.wait_ge(w_turned, BANKS)
            step(0, 0)
            with sp.Fori(0, TILES - 1) as t:
                step(t, 1)
                store_x(t + 1)
                step(t, 2)
                step(t, 3)
                step(t + 1, 0)
                store_y(t)
            step(TILES - 1, 1)
            step(TILES - 1, 2, ahead2=False)
            store_y(TILES - 1)
            sp.wait_ge(y_out, 16 * TILES)

        @block.gpsimd
        def _(pool):
            nc.gpsimd.memset(ident[:], 0.0).then_inc(ident_zero, 1)
            pool.wait_ge(ident_zero, 1)
            nc.gpsimd.affine_select(out=ident[:], in_=ident[:], compare_op=ALU.not_equal, fill=1.0, base=0,
                                    pattern=[[-1, P]], channel_multiplier=1).then_inc(ident_ready, 1)
            pool.wait_ge(ids_in, 16)
            for t in range(TILES):
                if t >= 1:
                    pool.wait_ge(x_turned, QH * t)
                for f in range(M):
                    nc.gpsimd.indirect_dma_start(
                        out=emb[:, f, :], out_offset=None, in_=tables[f],
                        in_offset=bass.IndirectOffsetOnAxis(ap=ids_sb[:, t, f:f + 1], axis=0)
                    ).then_inc(gathered, 16)

        @block.vector
        def _(dve):
            dve.wait_ge(w1_in, 16)

            def w1_run(first, count):
                return w1_raw[:, first:first + (count - 1) * (M + 1) + 1:M + 1]

            nc.vector.tensor_copy(w1_sym[:, 0:M], w1_run(0, M)).then_inc(w1_symmetric, 1)
            for k in range(1, SHIFTS):
                nc.vector.tensor_tensor(w1_sym[:, k * M:(k + 1) * M - k], w1_run(k, M - k), w1_run(k * M, M - k),
                                        ALU.add).then_inc(w1_symmetric, 1)
                nc.vector.tensor_tensor(w1_sym[:, (k + 1) * M - k:(k + 1) * M], w1_run((M - k) * M, k),
                                        w1_run(M - k, k), ALU.add).then_inc(w1_symmetric, 1)
            dve.wait_ge(w2_in, 16)
            for i in range(I // 2, I):
                pack_w2(nc.vector.tensor_copy, i).then_inc(w2_packed_dve, 1)
            for n in range(1, len(banks), 2):
                dve.wait_ge(w_turned, n + 1)
                nc.vector.tensor_copy(bank_dst(n), bank_src(n)).then_inc(w_copied_dve, 1)

            def products1(t, q):
                g, par = QN * t + q, q % 2
                dve.wait_ge(l1_in[par], 16 * (1 + L1_TILES) * (2 * t + q // 2 + 1))
                if not (isinstance(g, int) and g == 0):
                    dve.wait_ge(l1_done, g)
                for a, b, rows in ((0, 3, L1_ROWS), (3, 6, L1_ROWS), (6, 7, L1_LAST)):
                    nc.vector.tensor_tensor(
                        prod1[0:rows, a:b, :], l1_a[0:rows, par, None, :].to_broadcast([rows, b - a, N]),
                        l1_b[0:rows, par, a:b, :], ALU.mult).then_inc(prod1_ready, 1)

            def products2(t, q, k):
                g, par = QN * t + q, q % 2
                n = GROUPS * g + k
                slot = (GROUPS * q + k) % RING
                if k == 0:
                    dve.wait_ge(x1_rep_in[par], 16 * I * (2 * t + q // 2 + 1))
                    dve.wait_ge(x0_rep_in[par], 16 * (J + 1) * (2 * t + q // 2 + 1))
                if not (isinstance(n, int) and n < RING):
                    dve.wait_ge(l2_done, n - RING + 1)
                i, j = divmod(k, J // G3)
                if i < I:
                    a, b = x1_rep[:, par, i, None, :], x0_rep[:, par, G3 * j:G3 * (j + 1), :]
                else:
                    a, b = x1[:, q:q + 1, :, :].rearrange("s a d b -> s a (d b)"), x0_rep[:, par, J:XB, :]
                nc.vector.tensor_tensor(prod2[:, slot], a.to_broadcast([P, G3, N]), b,
                                        ALU.mult).then_inc(prod2_ready, 1)

            def sum_d(dst, x, ready, count, done):
                dve.wait_ge(ready, count)
                nc.vector.tensor_reduce(dst[:], x[:].rearrange("s q d b -> s b (q d)"), AX_X,
                                        ALU.add).then_inc(done, 1)

            def step(t, q, ahead=True):
                if ahead:
                    t1, q1 = (t, q + 1) if q + 1 < QN else (t + 1, 0)
                    products1(t1, q1)
                for k in range(GROUPS):
                    products2(t, q, k)
                    if q == 2 and k == 6:
                        sum_d(p1, x1, x1_ready, QN * (t + 1), p1_ready)
                    if q == 0 and k == 3 and not (isinstance(t, int) and t == 0):
                        sum_d(p2, x2, x2_ready, QN * t, p2_ready)

            products1(0, 0)
            dve.wait_ge(w_turned, BANKS)
            step(0, 0)
            with dve.Fori(0, TILES - 1) as t:
                step(t, 1)
                step(t, 2)
                step(t, 3)
                step(t + 1, 0)
            step(TILES - 1, 1)
            step(TILES - 1, 2)
            step(TILES - 1, 3, ahead=False)
            sum_d(p2, x2, x2_ready, CHUNKS, p2_ready)

        @block.scalar
        def _(act):
            act.wait_ge(w2_in, 16)
            for i in range(I // 2):
                pack_w2(nc.scalar.copy, i).then_inc(w2_packed_act, 1)
            for n in range(0, len(banks), 2):
                act.wait_ge(w_turned, n + 1)
                nc.scalar.copy(bank_dst(n), bank_src(n)).then_inc(w_copied_act, 1)
            act.wait_ge(w_turned, BANKS)
            nc.scalar.copy(denseT[:], tr_ps[(BANKS - 1) % 2][0:DENSE, 0:TILES * P]).then_inc(w_copied_act, 1)
            act.wait_ge(small_in, 16 * SMALL)

            def copy_x(t):
                for k in range(QH):
                    act.wait_ge(x_turned, QH * t + k + 1)
                    if k == 0 and not (isinstance(t, int) and t == 0):
                        act.wait_ge(x_scratched, 16 * 2 * QH * t)
                    nc.scalar.copy(xT[:, k, :], tr_ps[k % 2][0:DH * M, :]).then_inc(x_copied, 1)

            def finish_x1(t, q):
                act.wait_ge(l1_done, QN * t + q + 1)
                nc.scalar.activation(x1[:, q, :, :].rearrange("s d b -> s (d b)"), x1_ps[q % 2][:], ACT.Relu,
                                     bias=b1_sb[:, 0:1]).then_inc(x1_ready, 1)

            def finish_x2(t, q):
                act.wait_ge(l2_done, GROUPS * (QN * t + q + 1))
                nc.scalar.activation(x2[:, q, :, :].rearrange("s d b -> s (d b)"), x2_ps[q % 2][:], ACT.Relu,
                                     bias=b2_sb[:, 0:1]).then_inc(x2_ready, 1)

            def mlp(t):
                act.wait_ge(h1_summed, t + 1)
                for o in range(O1):
                    nc.scalar.activation(h1[:, o, :], h_ps[:, o * P:(o + 1) * P], ACT.Relu,
                                         bias=bt1[:, o:o + 1]).then_inc(h1_ready, 1)
                act.wait_ge(h2_summed, t + 1)
                for o in range(O2):
                    nc.scalar.activation(h2[:, o, :], h_ps[:, o * P:(o + 1) * P], ACT.Relu,
                                         bias=bt2[:, o:o + 1]).then_inc(h2_ready, 1)
                act.wait_ge(y_summed, t + 1)
                if not (isinstance(t, int) and t == 0):
                    act.wait_ge(y_out, 16 * t)
                nc.scalar.copy(y_sb[:], y_ps[0:1, 0:P]).then_inc(y_ready, 1)

            copy_x(0)
            finish_x1(0, 0)
            finish_x1(0, 1)
            finish_x2(0, 0)
            with act.Fori(0, TILES - 1) as t:
                finish_x1(t, 2)
                finish_x2(t, 1)
                copy_x(t + 1)
                finish_x1(t, 3)
                finish_x2(t, 2)
                finish_x1(t + 1, 0)
                finish_x2(t, 3)
                finish_x1(t + 1, 1)
                mlp(t)
                finish_x2(t + 1, 0)
            finish_x1(TILES - 1, 2)
            finish_x2(TILES - 1, 1)
            finish_x1(TILES - 1, 3)
            finish_x2(TILES - 1, 2)
            finish_x2(TILES - 1, 3)
            mlp(TILES - 1)

        @block.tensor
        def _(pe):
            pe.wait_ge(ident_ready, 1)

            def copied(n):
                if n % 2 == 0 or n == len(banks):
                    pe.wait_ge(w_copied_act, n // 2 + 1)
                else:
                    pe.wait_ge(w_copied_dve, n // 2 + 1)

            for n, bank in enumerate(banks):
                if n == 0:
                    pe.wait_ge(w1_symmetric, 2 * SHIFTS - 1)
                if n == 3:
                    pe.wait_ge(w2_packed_act, I // 2)
                    pe.wait_ge(w2_packed_dve, I // 2)
                if n >= 2:
                    copied(n - 2)
                for k, (_, src) in enumerate(bank):
                    last = nc.tensor.transpose(tr_ps[n % 2][0:heights[n], k * S:(k + 1) * S], src, ident[:])
                last.then_inc(w_turned, 1)
            pe.wait_ge(small_in, 16 * SMALL)
            copied(BANKS - 3)
            for t in range(TILES):
                last = nc.tensor.transpose(tr_ps[(BANKS - 1) % 2][0:DENSE, t * P:(t + 1) * P], dense_sb[:, t, :],
                                           ident[:])
            last.then_inc(w_turned, 1)
            copied(BANKS - 2)
            pe.wait_ge(w_copied_act, (len(banks) + 1) // 2 + 1)

            def turn_x(t):
                pe.wait_ge(gathered, 16 * M * (t + 1))
                for k in range(QH):
                    for d in range(DQ):
                        src = emb[:].rearrange("b f (e d) -> b (f e) d", e=DH)[:, :, k * DQ + d]
                        last = nc.tensor.transpose(tr_ps[k][0:DH * M, d * P:(d + 1) * P], src, ident[:])
                    last.then_inc(x_turned, 1)

            def layer1(t, q):
                g = QN * t + q
                if not (isinstance(g, int) and g < 2):
                    pe.wait_ge(x1_ready, g - 1)
                for j in range(L1_TILES):
                    rows = L1_ROWS if j < L1_TILES - 1 else L1_LAST
                    if j % 3 == 0:
                        pe.wait_ge(prod1_ready, 3 * g + j // 3 + 1)
                    last = nc.tensor.matmul(x1_ps[q % 2][:], w1T[0:rows, j, :], prod1[0:rows, j, :],
                                            start=(j == 0), stop=(j == L1_TILES - 1))
                last.then_inc(l1_done, 1)

            def layer2(t, q, k):
                g = QN * t + q
                slot = (GROUPS * q + k) % RING
                if k == 0 and not (isinstance(g, int) and g < 2):
                    pe.wait_ge(x2_ready, g - 1)
                pe.wait_ge(prod2_ready, GROUPS * g + k + 1)
                for c in range(G3):
                    n = k * G3 + c
                    last = nc.tensor.matmul(x2_ps[q % 2][:], w2T[:, n, :], prod2[:, slot, c, :],
                                            start=(n == 0), stop=(n == L2_TILES - 1))
                last.then_inc(l2_done, 1)

            def mlp_h1(t):
                pe.wait_ge(p1_ready, t + 1)
                pe.wait_ge(p2_ready, t + 1)
                for o in range(O1):
                    cols = slice(o * P, (o + 1) * P)
                    nc.tensor.matmul(h_ps[:, cols], wt1a[:, 0, cols], p1[:], start=True, stop=False)
                    nc.tensor.matmul(h_ps[:, cols], wt1a[:, 1, cols], p2[:], start=False, stop=False)
                    dT = denseT[:, t * P:(t + 1) * P] if isinstance(t, int) else denseT[:, bass.ts(t, P)]
                    last = nc.tensor.matmul(h_ps[:, cols], wt1b[:, cols], dT, start=False, stop=True)
                last.then_inc(h1_summed, 1)

            def mlp_h2(t):
                pe.wait_ge(h1_ready, O1 * (t + 1))
                for o in range(O2):
                    cols = slice(o * P, (o + 1) * P)
                    for k in range(O1):
                        last = nc.tensor.matmul(h_ps[:, cols], wt2[:, k, cols], h1[:, k, :],
                                                start=(k == 0), stop=(k == O1 - 1))
                last.then_inc(h2_summed, 1)

            def mlp_y(t):
                pe.wait_ge(h2_ready, O2 * (t + 1))
                for k in range(O2):
                    last = nc.tensor.matmul(y_ps[0:1, 0:P], wt3[:, k, :], h2[:, k, :],
                                            start=(k == 0), stop=(k == O2 - 1))
                last.then_inc(y_summed, 1)

            def step(t, q, ahead=True, mlp_of=None):
                if ahead:
                    t1, q1 = (t, q + 1) if q + 1 < QN else (t + 1, 0)
                    layer1(t1, q1)
                for k in range(GROUPS):
                    layer2(t, q, k)
                    if mlp_of is not None:
                        if k == 6:
                            mlp_h1(mlp_of)
                        if k == 8:
                            mlp_h2(mlp_of)
                        if k == 10:
                            mlp_y(mlp_of)

            turn_x(0)
            layer1(0, 0)
            step(0, 0)
            with pe.Fori(0, TILES - 1) as t:
                step(t, 1)
                turn_x(t + 1)
                step(t, 2)
                step(t, 3)
                step(t + 1, 0, mlp_of=t)
            step(TILES - 1, 1)
            step(TILES - 1, 2)
            step(TILES - 1, 3, ahead=False)
            mlp_h1(TILES - 1)
            mlp_h2(TILES - 1)
            mlp_y(TILES - 1)


_INS = (["dense_ctx", "ids"] + [f"tbl_{f}" for f in range(M)]
        + ["W_top1", "b_top1", "W_top2", "b_top2", "W_top3", "L0_rec_W1", "L0_rec_b1", "L0_rec_W2", "L0_rec_b2"])


def kernel(**inputs):
    import numpy as _np
    import concourse.bacc as _bacc
    from concourse.bass_utils import run_bass_kernel_spmd as _run

    nc = _bacc.Bacc("TRN2", target_bir_lowering=False, num_devices=1)
    arrays, args = {}, []
    for name in _INS:
        a = _np.ascontiguousarray(inputs[name])
        arrays[f"in_{name}_dram"] = a
        args.append(nc.dram_tensor(f"in_{name}_dram", a.shape, mybir.dt.from_np(a.dtype), kind="ExternalInput").ap())
    out = nc.dram_tensor("out_0_dram", (B, 1), F32, kind="ExternalOutput").ap()
    build(nc, args[0], args[1], args[2:2 + M], *args[2 + M:], out)
    r = _run(nc, [arrays], core_ids=[0])
    return r.results[0]["out_0_dram"]
```

```python
from contextlib import ExitStack

import concourse.bass as bass
from concourse import mybir

ALU = mybir.AluOpType
ACT = mybir.ActivationFunctionType
AX_X = mybir.AxisListType.X
F32 = mybir.dt.float32
F32R = mybir.dt.float32r
I32 = mybir.dt.int32

P = 128
B, M, D = 512, 39, 16
S = 128
TILES = B // P
QN = 4
DH = 2
DQ = D // QN
QH = QN // DH
N = DQ * P
CHUNKS = TILES * QN

SHIFTS = (M + 1) // 2
KG = P // M
L1_ROWS = KG * M
L1_TILES = -(-SHIFTS // KG)
L1_LAST = (SHIFTS - KG * (L1_TILES - 1)) * M
X_ROWS = M + KG * L1_TILES - 1

MG = 4
HG = P // MG
J = M // MG
I = S // HG
SINGLE = M - MG * J
L2_TILES = I * J + SINGLE
XB = J + SINGLE
G3 = 3
JG = J // G3
GROUPS = L2_TILES // G3
SPLIT = [1, 3, 5, 7, 9, 11]
WHOLE = [k for k in range(GROUPS) if k not in SPLIT]
WHOLE_RING = 4
SPLIT_RING = 2

H1, H2 = 512, 256
O1, O2 = H1 // P, H2 // P
DENSE = 16
SMALL = 6 + 2 * O2 + O1


def in_register(engine, value):
    return value if isinstance(value, int) else engine.snap(value)


def build(nc, dense_ctx, ids, tables, W_top1, b_top1, W_top2, b_top2, W_top3, W1, b1, W2, b2, out):
    assert SHIFTS // L1_TILES == L1_LAST // M and J % G3 == 0 and SINGLE == G3 and L2_TILES % G3 == 0
    assert 0 in WHOLE and GROUPS - 1 in WHOLE
    assert QN * len(WHOLE) % WHOLE_RING == 0 and QN * len(SPLIT) % SPLIT_RING == 0

    with ExitStack() as ctx:
        def sb(name, shape, dt=F32):
            return ctx.enter_context(nc.sbuf_tensor(name, shape, dt))

        def ps(name, shape):
            return ctx.enter_context(nc.psum_tensor(name, shape, F32))

        def sem(name):
            return ctx.enter_context(nc.semaphore(name))

        x_scratch = nc.dram_tensor("x_scratch", [CHUNKS, X_ROWS, N], F32)
        x1_scratch = nc.dram_tensor("x1_scratch", [2, S, N], F32)

        ident = sb("ident", [P, P])
        ids_sb = sb("ids_sb", [P, TILES, M], I32)
        dense_sb = sb("dense_sb", [P, TILES, DENSE])
        denseT = sb("denseT", [DENSE, TILES * P])
        emb = sb("emb", [P, M, D])
        xT = sb("xT", [DH * M, QN // DH, N])
        w1T = sb("w1T", [P, L1_TILES, S])
        w2T = sb("w2T", [P, len(WHOLE), G3, S])
        w2H = sb("w2H", [P, len(SPLIT), G3, S], F32R)
        w2L = sb("w2L", [P, len(SPLIT), G3, S], F32R)
        b1_sb = sb("b1_sb", [S, 1])
        b2_sb = sb("b2_sb", [S, 1])
        wt1a = sb("wt1a", [P, 2, H1])
        wt1b = sb("wt1b", [DENSE, H1])
        wt2 = sb("wt2", [P, O1, H2])
        wt3 = sb("wt3", [P, O2, 1])
        bt1 = sb("bt1", [P, O1])
        bt2 = sb("bt2", [P, O2])

        l1_a = sb("l1_a", [P, N])
        l1_b = sb("l1_b", [P, L1_TILES, N])
        prod1 = sb("prod1", [P, L1_TILES, N])
        x0_rep = sb("x0_rep", [P, XB, N])
        x1_rep = sb("x1_rep", [P, 2, I, N])
        whole = sb("whole", [P, WHOLE_RING, G3, N])
        to_split = sb("to_split", [P, SPLIT_RING, G3, N])
        high = sb("high", [P, SPLIT_RING, G3, N], F32R)
        low = sb("low", [P, SPLIT_RING, G3, N], F32R)
        x1 = sb("x1", [S, QN, DQ, P])
        x2 = sb("x2", [S, QN, DQ, P])
        p1 = sb("p1", [S, P])
        p2 = sb("p2", [S, 2, P])
        h1 = sb("h1", [P, O1, P])
        h2 = sb("h2", [P, O2, P])
        y_sb = sb("y_sb", [1, P])
        w2_raw = x0_rep[:].rearrange("p a n -> p (a n)")[:, 0:S * M].rearrange("p (h m) -> p h m", m=M)
        w2_packed = whole[:].rearrange("p a c n -> p (a c n)")[:, 0:I * J * P]
        w1_sym = x0_rep[:].rearrange("p a n -> p (a n)")[:, S * M:S * M + SHIFTS * M]
        w1_raw = x1_rep[:, 1, :, :].rearrange("p a n -> p (a n)")[:, 0:M * M]

        x1_ps = [ps(f"x1_ps{i}", [P, N]) for i in range(2)]
        x2_ps = [ps(f"x2_ps{i}", [P, N]) for i in range(2)]
        tr_ps = [ps(f"tr_ps{i}", [P, N]) for i in range(2)]
        h_ps = ps("h_ps", [P, N])
        y_ps = ps("y_ps", [P, N])

        ids_in = sem("ids_in")
        w1_in = sem("w1_in")
        w2_in = sem("w2_in")
        small_in = sem("small_in")
        ident_zero = sem("ident_zero")
        ident_ready = sem("ident_ready")
        gathered = sem("gathered")
        w1_symmetric = sem("w1_symmetric")
        w2_packed_act = sem("w2_packed_act")
        w2_packed_dve = sem("w2_packed_dve")
        w_turned = sem("w_turned")
        w_copied = sem("w_copied")
        w_low = sem("w_low")
        x_turned = sem("x_turned")
        x_copied = sem("x_copied")
        x_scratched = sem("x_scratched")
        l1_in = sem("l1_in")
        x0_rep_in = [sem(f"x0_rep_in{j}") for j in range(JG + 1)]
        x1_rep_in = [sem(f"x1_rep_in{i}") for i in range(2)]
        prod1_ready = sem("prod1_ready")
        l1_done = sem("l1_done")
        x1_ready = sem("x1_ready")
        x1_scratched = sem("x1_scratched")
        prod2_made = sem("prod2_made")
        high_ready = sem("high_ready")
        low_ready = sem("low_ready")
        whole_used = sem("whole_used")
        split_used = sem("split_used")
        x2_ready = sem("x2_ready")
        p1_ready = sem("p1_ready")
        p2_ready = sem("p2_ready")
        h1_summed = sem("h1_summed")
        h1_ready = sem("h1_ready")
        h2_summed = sem("h2_summed")
        h2_ready = sem("h2_ready")
        y_summed = sem("y_summed")
        y_ready = sem("y_ready")
        y_out = sem("y_out")

        w1_tiles = [w1_sym[:, j * L1_ROWS:min((j + 1) * L1_ROWS, SHIFTS * M)] for j in range(L1_TILES)]
        w2_tiles = [w2_packed[:, n * P:(n + 1) * P] for n in range(I * J)]
        w2_tiles += [w2_raw[:, :, J * MG + n] for n in range(SINGLE)]
        banks = [w1_tiles[0:3], w1_tiles[3:6], w1_tiles[6:7]]
        banks += [w2_tiles[n:n + G3] for n in range(0, L2_TILES, G3)]
        heights = [L1_ROWS, L1_ROWS, L1_LAST] + [P] * GROUPS

        def pack_w2(engine_copy, k):
            g, i = divmod(k, I)
            dst = w2_packed[:, k * G3 * P:(k + 1) * G3 * P].rearrange("s (c a h) -> s c a h", c=G3, a=MG)
            src = w2_raw[:, i:S:I, 0:J * MG].rearrange("s h (a g c) -> s g c a h", a=MG, c=G3)[:, g]
            return engine_copy(dst, src)

        def bank_dst(n):
            if n < 3:
                return w1T[0:heights[n], 3 * n:3 * n + len(banks[n]), :]
            return w2H[:, SPLIT.index(n - 3)] if n - 3 in SPLIT else w2T[:, WHOLE.index(n - 3)]

        def bank_src(n):
            return tr_ps[n % 2][0:heights[n], 0:len(banks[n]) * S].rearrange("p (k s) -> p k s", s=S)

        BANKS = len(banks) + 1

        block = ctx.enter_context(nc.Block())

        @block.sync
        def _(sp):
            sp.dma_start(ids_sb[:], ids.rearrange("(t p) f -> p t f", p=P)).then_inc(ids_in, 16)
            sp.dma_start(w1_raw, W1.rearrange("s h m -> s (h m)")).then_inc(w1_in, 16)
            sp.dma_start(w2_raw, W2).then_inc(w2_in, 16)
            sp.dma_start(dense_sb[:], dense_ctx.rearrange("(t p) c -> p t c", p=P)).then_inc(small_in, 16)
            sp.dma_start(b1_sb[:], b1.rearrange("(s a) -> s a", a=1)).then_inc(small_in, 16)
            sp.dma_start(b2_sb[:], b2.rearrange("(s a) -> s a", a=1)).then_inc(small_in, 16)
            sp.dma_start(wt1a[:], W_top1[0:2 * P, :].rearrange("(k p) n -> p k n", p=P)).then_inc(small_in, 16)
            sp.dma_start(wt1b[:], W_top1[2 * P:2 * P + DENSE, :]).then_inc(small_in, 16)
            sp.dma_start(wt2[:], W_top2.rearrange("(k p) n -> p k n", p=P)).then_inc(small_in, 16)
            for vector, columns in ((W_top3.rearrange("k a -> (k a)"), wt3[:, :, 0]), (b_top1, bt1), (b_top2, bt2)):
                for k in range(vector.shape[0] // P):
                    sp.dma_start(columns[:, k:k + 1], vector[k * P:(k + 1) * P].rearrange("(p a) -> p a", a=1)
                                 ).then_inc(small_in, 16)

            def store_x(t):
                at = [in_register(sp, (QN * t * X_ROWS + r0) * N) for r0 in (0, M)]
                sp.wait_ge(x_copied, QH * (t + 1))
                for base, rows in zip(at, (M, X_ROWS - M)):
                    for k in range(QH):
                        dst = bass.AP(x_scratch, base + k * X_ROWS * N, [[N, rows], [QH * X_ROWS * N, DH], [1, N]])
                        sp.dma_start(dst, xT[0:DH * rows, k, :]).then_inc(x_scratched, 16)

            def load_l1(t, q):
                g = QN * t + q
                base = in_register(sp, g * X_ROWS * N)
                if q == 0:
                    sp.wait_ge(x_scratched, 16 * 2 * QH * (t + 1))
                sp.dma_start(l1_a[0:L1_ROWS, :],
                             bass.AP(x_scratch, base, [[0, KG], [N, M], [1, N]])).then_inc(l1_in, 16)
                sp.dma_start(l1_b[0:L1_ROWS, :, :],
                             bass.AP(x_scratch, base, [[L1_TILES * N, KG], [N, M], [1, L1_TILES * N]])
                             ).then_inc(l1_in, 16)

            def load_x0_rep(t, q, j):
                g = QN * t + q
                base = in_register(sp, g * X_ROWS * N)
                if not (isinstance(g, int) and g == 0):
                    used = GROUPS * (g - 1) + (I * (j + 1) if j < JG else GROUPS)
                    sp.wait_ge(prod2_made, used)
                if j < JG:
                    at, src = G3 * j * N, [[J * N, MG], [0, HG], [1, G3 * N]]
                else:
                    at, src = MG * J * N, [[0, P], [1, SINGLE * N]]
                sp.dma_start(x0_rep[:, G3 * j:G3 * (j + 1), :],
                             bass.AP(x_scratch, base + at, src)).then_inc(x0_rep_in[j], 16)

            def repeat_x1(t, q):
                g, par = QN * t + q, q % 2
                sp.wait_ge(x1_ready, g + 1)
                sp.dma_start(x1_scratch[par], x1[:, q, :, :].rearrange("s d b -> s (d b)")).then_inc(x1_scratched, 16)
                sp.wait_ge(x1_scratched, 16 * (g + 1))
                sp.dma_start(x1_rep[:, par, :, :],
                             bass.AP(x1_scratch, par * S * N, [[0, MG], [I * N, HG], [1, I * N]])
                             ).then_inc(x1_rep_in[par], 16)

            def step(t, q, ahead=True, ahead2=True):
                t1, q1 = (t, q + 1) if q + 1 < QN else (t + 1, 0)
                t2, q2 = (t, q + 2) if q + 2 < QN else (t + 1, q + 2 - QN)
                if ahead:
                    repeat_x1(t1, q1)
                if ahead2:
                    load_l1(t2, q2)
                if ahead:
                    for j in range(JG + 1):
                        load_x0_rep(t1, q1, j)

            def store_y(t):
                at = in_register(sp, P * t)
                sp.wait_ge(y_ready, t + 1)
                sp.dma_start(bass.AP(out.tensor, at, [[P, 1], [1, P]]), y_sb[:]).then_inc(y_out, 16)

            store_x(0)
            load_l1(0, 0)
            sp.wait_ge(w_turned, BANKS)
            for j in range(JG + 1):
                load_x0_rep(0, 0, j)
            sp.wait_ge(prod1_ready, 3)
            load_l1(0, 1)
            repeat_x1(0, 0)
            step(0, 0)
            with sp.Fori(0, TILES - 1) as t:
                step(t, 1)
                store_x(t + 1)
                step(t, 2)
                step(t, 3)
                step(t + 1, 0)
                store_y(t)
            step(TILES - 1, 1)
            step(TILES - 1, 2, ahead2=False)
            store_y(TILES - 1)
            sp.wait_ge(y_out, 16 * TILES)

        @block.gpsimd
        def _(pool):
            nc.gpsimd.memset(ident[:], 0.0).then_inc(ident_zero, 1)
            pool.wait_ge(ident_zero, 1)
            nc.gpsimd.affine_select(out=ident[:], in_=ident[:], compare_op=ALU.not_equal, fill=1.0, base=0,
                                    pattern=[[-1, P]], channel_multiplier=1).then_inc(ident_ready, 1)
            pool.wait_ge(ids_in, 16)
            for t in range(TILES):
                if t >= 1:
                    pool.wait_ge(x_turned, QH * t)
                for f in range(M):
                    nc.gpsimd.indirect_dma_start(
                        out=emb[:, f, :], out_offset=None, in_=tables[f],
                        in_offset=bass.IndirectOffsetOnAxis(ap=ids_sb[:, t, f:f + 1], axis=0)
                    ).then_inc(gathered, 16)

        @block.vector
        def _(dve):
            dve.wait_ge(w1_in, 16)

            def w1_run(first, count):
                return w1_raw[:, first:first + (count - 1) * (M + 1) + 1:M + 1]

            nc.vector.tensor_copy(w1_sym[:, 0:M], w1_run(0, M)).then_inc(w1_symmetric, 1)
            for k in range(1, SHIFTS):
                at = (k % L1_TILES * KG + k // L1_TILES) * M
                nc.vector.tensor_tensor(w1_sym[:, at:at + M - k], w1_run(k, M - k), w1_run(k * M, M - k),
                                        ALU.add).then_inc(w1_symmetric, 1)
                nc.vector.tensor_tensor(w1_sym[:, at + M - k:at + M], w1_run((M - k) * M, k),
                                        w1_run(M - k, k), ALU.add).then_inc(w1_symmetric, 1)
            dve.wait_ge(w2_in, 16)
            for k in range(I * JG // 2, I * JG):
                pack_w2(nc.vector.tensor_copy, k).then_inc(w2_packed_dve, 1)
            for b, k in enumerate(SPLIT):
                dve.wait_ge(w_copied, k + 3 + 1)
                nc.vector.tensor_tensor(w2L[:, b], bank_src(k + 3), w2H[:, b].bitcast(F32),
                                        ALU.subtract).then_inc(w_low, 1)

            def products1(t, q):
                g = QN * t + q
                if not (isinstance(g, int) and g == 0):
                    dve.wait_ge(l1_done, g)
                dve.wait_ge(l1_in, 16 * 2 * (g + 1))
                for a, b, rows in ((0, 3, L1_ROWS), (3, 6, L1_ROWS), (6, 7, L1_LAST)):
                    nc.vector.tensor_tensor(
                        prod1[0:rows, a:b, :], l1_a[0:rows, None, :].to_broadcast([rows, b - a, N]),
                        l1_b[0:rows, a:b, :], ALU.mult).then_inc(prod1_ready, 1)

            def product2(t, q, k):
                g, par = QN * t + q, q % 2
                j, i = divmod(k, I)
                if k == 0:
                    dve.wait_ge(x1_rep_in[par], 16 * (2 * t + q // 2 + 1))
                if i == 0:
                    dve.wait_ge(x0_rep_in[j], 16 * (g + 1))
                if k in WHOLE:
                    n = len(WHOLE) * g + WHOLE.index(k)
                    dst = whole[:, (len(WHOLE) * q + WHOLE.index(k)) % WHOLE_RING]
                    if not (isinstance(n, int) and n < WHOLE_RING):
                        dve.wait_ge(whole_used, n - WHOLE_RING + 1)
                else:
                    n = len(SPLIT) * g + SPLIT.index(k)
                    dst = to_split[:, (len(SPLIT) * q + SPLIT.index(k)) % SPLIT_RING]
                    if not (isinstance(n, int) and n < SPLIT_RING):
                        dve.wait_ge(low_ready, n - SPLIT_RING + 1)
                a = x1_rep[:, par, i, None, :] if j < JG else x1[:, q:q + 1, :, :].rearrange("s a d b -> s a (d b)")
                nc.vector.tensor_tensor(dst, a.to_broadcast([P, G3, N]), x0_rep[:, G3 * j:G3 * (j + 1), :],
                                        ALU.mult).then_inc(prod2_made, 1)

            def low_part(t, q, k):
                b = SPLIT.index(k)
                n = len(SPLIT) * (QN * t + q) + b
                slot = (len(SPLIT) * q + b) % SPLIT_RING
                dve.wait_ge(high_ready, n + 1)
                nc.vector.tensor_tensor(low[:, slot], to_split[:, slot], high[:, slot].bitcast(F32),
                                        ALU.subtract).then_inc(low_ready, 1)

            def sum_d(dst, x, done):
                nc.vector.tensor_reduce(dst, x.rearrange("s q d b -> s b (q d)"), AX_X, ALU.add).then_inc(done, 1)

            def step(t, q, ahead=True):
                if ahead:
                    t1, q1 = (t, q + 1) if q + 1 < QN else (t + 1, 0)
                    products1(t1, q1)
                for k in range(GROUPS):
                    product2(t, q, k)
                    if k - 1 in SPLIT:
                        low_part(t, q, k - 1)
                    if q == 2 and k == 6:
                        dve.wait_ge(x1_ready, QN * (t + 1))
                        sum_d(p1[:], x1[:], p1_ready)
                    if q == 3 and k == 6:
                        dve.wait_ge(x2_ready, QN * t + 3)
                        sum_d(p2[:, 0, :], x2[:, 0:3], p2_ready)
                    if q == 0 and k == 3 and not (isinstance(t, int) and t == 0):
                        dve.wait_ge(x2_ready, QN * t)
                        sum_d(p2[:, 1, :], x2[:, 3:4], p2_ready)

            products1(0, 0)
            dve.wait_ge(w_turned, BANKS)
            step(0, 0)
            with dve.Fori(0, TILES - 1) as t:
                step(t, 1)
                step(t, 2)
                step(t, 3)
                step(t + 1, 0)
            step(TILES - 1, 1)
            step(TILES - 1, 2)
            step(TILES - 1, 3, ahead=False)
            dve.wait_ge(x2_ready, CHUNKS)
            sum_d(p2[:, 1, :], x2[:, 3:4], p2_ready)

        @block.scalar
        def _(act):
            act.wait_ge(w2_in, 16)
            for k in range(I * JG // 2):
                pack_w2(nc.scalar.copy, k).then_inc(w2_packed_act, 1)
            for n in range(len(banks)):
                act.wait_ge(w_turned, n + 1)
                nc.scalar.copy(bank_dst(n), bank_src(n)).then_inc(w_copied, 1)
            act.wait_ge(w_turned, BANKS)
            nc.scalar.copy(denseT[:], tr_ps[(BANKS - 1) % 2][0:DENSE, 0:TILES * P]).then_inc(w_copied, 1)
            act.wait_ge(small_in, 16 * SMALL)

            def copy_x(t):
                for k in range(QH):
                    act.wait_ge(x_turned, QH * t + k + 1)
                    if k == 0 and not (isinstance(t, int) and t == 0):
                        act.wait_ge(x_scratched, 16 * 2 * QH * t)
                    nc.scalar.copy(xT[:, k, :], tr_ps[k % 2][0:DH * M, :]).then_inc(x_copied, 1)

            def finish_x1(t, q):
                act.wait_ge(l1_done, QN * t + q + 1)
                nc.scalar.activation(x1[:, q, :, :].rearrange("s d b -> s (d b)"), x1_ps[q % 2][:], ACT.Relu,
                                     bias=b1_sb[:, 0:1]).then_inc(x1_ready, 1)

            def finish_x2(t, q):
                act.wait_ge(whole_used, len(WHOLE) * (QN * t + q + 1))
                nc.scalar.activation(x2[:, q, :, :].rearrange("s d b -> s (d b)"), x2_ps[q % 2][:], ACT.Relu,
                                     bias=b2_sb[:, 0:1]).then_inc(x2_ready, 1)

            def high_part(t, q, k):
                b = SPLIT.index(k)
                n = len(SPLIT) * (QN * t + q) + b
                if not (isinstance(n, int) and n < SPLIT_RING):
                    act.wait_ge(split_used, n - SPLIT_RING + 1)
                act.wait_ge(prod2_made, GROUPS * (QN * t + q) + k + 1)
                slot = (len(SPLIT) * q + b) % SPLIT_RING
                nc.scalar.copy(high[:, slot], to_split[:, slot]).then_inc(high_ready, 1)

            def mlp_h1(t):
                act.wait_ge(h1_summed, t + 1)
                for o in range(O1):
                    nc.scalar.activation(h1[:, o, :], h_ps[:, o * P:(o + 1) * P], ACT.Relu,
                                         bias=bt1[:, o:o + 1]).then_inc(h1_ready, 1)

            def mlp_h2(t):
                act.wait_ge(h2_summed, t + 1)
                for o in range(O2):
                    nc.scalar.activation(h2[:, o, :], h_ps[:, o * P:(o + 1) * P], ACT.Relu,
                                         bias=bt2[:, o:o + 1]).then_inc(h2_ready, 1)

            def mlp_y(t):
                act.wait_ge(y_summed, t + 1)
                if not (isinstance(t, int) and t == 0):
                    act.wait_ge(y_out, 16 * t)
                nc.scalar.copy(y_sb[:], y_ps[0:1, 0:P]).then_inc(y_ready, 1)

            def step(t, q, ahead=True, mlp_of=None):
                for k in SPLIT:
                    high_part(t, q, k)
                    if ahead and k == SPLIT[0]:
                        t1, q1 = (t, q + 1) if q + 1 < QN else (t + 1, 0)
                        finish_x1(t1, q1)
                    if mlp_of is not None and k == 7:
                        mlp_h1(mlp_of)
                if mlp_of is not None:
                    mlp_h2(mlp_of)
                    mlp_y(mlp_of)
                finish_x2(t, q)

            copy_x(0)
            finish_x1(0, 0)
            step(0, 0)
            with act.Fori(0, TILES - 1) as t:
                step(t, 1)
                copy_x(t + 1)
                step(t, 2)
                step(t, 3)
                step(t + 1, 0, mlp_of=t)
            step(TILES - 1, 1)
            step(TILES - 1, 2)
            step(TILES - 1, 3, ahead=False)
            mlp_h1(TILES - 1)
            mlp_h2(TILES - 1)
            mlp_y(TILES - 1)

        @block.tensor
        def _(pe):
            pe.wait_ge(ident_ready, 1)

            def copied(n):
                pe.wait_ge(w_copied, n + 1)
                if n - 3 in SPLIT:
                    pe.wait_ge(w_low, SPLIT.index(n - 3) + 1)

            for n, bank in enumerate(banks):
                if n == 0:
                    pe.wait_ge(w1_symmetric, 2 * SHIFTS - 1)
                if n == 3:
                    pe.wait_ge(w2_packed_act, I * JG // 2)
                    pe.wait_ge(w2_packed_dve, I * JG - I * JG // 2)
                if n >= 2:
                    copied(n - 2)
                for k, src in enumerate(bank):
                    last = nc.tensor.transpose(tr_ps[n % 2][0:heights[n], k * S:(k + 1) * S], src, ident[:])
                last.then_inc(w_turned, 1)
            pe.wait_ge(small_in, 16 * SMALL)
            copied(BANKS - 3)
            for t in range(TILES):
                last = nc.tensor.transpose(tr_ps[(BANKS - 1) % 2][0:DENSE, t * P:(t + 1) * P], dense_sb[:, t, :],
                                           ident[:])
            last.then_inc(w_turned, 1)
            copied(BANKS - 2)
            copied(BANKS - 1)

            def turn_x(t):
                pe.wait_ge(gathered, 16 * M * (t + 1))
                for k in range(QH):
                    for d in range(DQ):
                        src = emb[:].rearrange("b f (e d) -> b (f e) d", e=DH)[:, :, k * DQ + d]
                        last = nc.tensor.transpose(tr_ps[k][0:DH * M, d * P:(d + 1) * P], src, ident[:])
                    last.then_inc(x_turned, 1)

            def layer1(t, q):
                g = QN * t + q
                if not (isinstance(g, int) and g < 2):
                    pe.wait_ge(x1_ready, g - 1)
                for j in range(L1_TILES):
                    rows = L1_ROWS if j < L1_TILES - 1 else L1_LAST
                    if j % 3 == 0:
                        pe.wait_ge(prod1_ready, 3 * g + j // 3 + 1)
                    last = nc.tensor.matmul(x1_ps[q % 2][:], w1T[0:rows, j, :], prod1[0:rows, j, :],
                                            start=(j == 0), stop=(j == L1_TILES - 1))
                last.then_inc(l1_done, 1)

            def layer2(t, q, k):
                g = QN * t + q
                acc = x2_ps[q % 2][:]
                if k == 0 and not (isinstance(g, int) and g < 2):
                    pe.wait_ge(x2_ready, g - 1)
                if k in WHOLE:
                    a = WHOLE.index(k)
                    slot = (len(WHOLE) * q + a) % WHOLE_RING
                    pe.wait_ge(prod2_made, GROUPS * g + k + 1)
                    for c in range(G3):
                        last = nc.tensor.matmul(acc, w2T[:, a, c, :], whole[:, slot, c, :],
                                                start=(k == 0 and c == 0), stop=(k == GROUPS - 1 and c == G3 - 1))
                    last.then_inc(whole_used, 1)
                else:
                    b = SPLIT.index(k)
                    slot = (len(SPLIT) * q + b) % SPLIT_RING
                    pe.wait_ge(high_ready, len(SPLIT) * g + b + 1)
                    for c in range(G3):
                        nc.tensor.matmul(acc, w2L[:, b, c, :], high[:, slot, c, :], start=False, stop=False)
                        nc.tensor.matmul(acc, w2H[:, b, c, :], high[:, slot, c, :], start=False, stop=False)
                    pe.wait_ge(low_ready, len(SPLIT) * g + b + 1)
                    for c in range(G3):
                        last = nc.tensor.matmul(acc, w2H[:, b, c, :], low[:, slot, c, :], start=False, stop=False)
                    last.then_inc(split_used, 1)

            def mlp_h1(t):
                pe.wait_ge(p1_ready, t + 1)
                pe.wait_ge(p2_ready, 2 * (t + 1))
                for o in range(O1):
                    cols = slice(o * P, (o + 1) * P)
                    nc.tensor.matmul(h_ps[:, cols], wt1a[:, 0, cols], p1[:], start=True, stop=False)
                    nc.tensor.matmul(h_ps[:, cols], wt1a[:, 1, cols], p2[:, 0, :], start=False, stop=False)
                    nc.tensor.matmul(h_ps[:, cols], wt1a[:, 1, cols], p2[:, 1, :], start=False, stop=False)
                    dT = denseT[:, t * P:(t + 1) * P] if isinstance(t, int) else denseT[:, bass.ts(t, P)]
                    last = nc.tensor.matmul(h_ps[:, cols], wt1b[:, cols], dT, start=False, stop=True)
                last.then_inc(h1_summed, 1)

            def mlp_h2(t):
                pe.wait_ge(h1_ready, O1 * (t + 1))
                for o in range(O2):
                    cols = slice(o * P, (o + 1) * P)
                    for k in range(O1):
                        last = nc.tensor.matmul(h_ps[:, cols], wt2[:, k, cols], h1[:, k, :],
                                                start=(k == 0), stop=(k == O1 - 1))
                last.then_inc(h2_summed, 1)

            def mlp_y(t):
                pe.wait_ge(h2_ready, O2 * (t + 1))
                for k in range(O2):
                    last = nc.tensor.matmul(y_ps[0:1, 0:P], wt3[:, k, :], h2[:, k, :],
                                            start=(k == 0), stop=(k == O2 - 1))
                last.then_inc(y_summed, 1)

            def step(t, q, ahead=True, mlp_of=None):
                if ahead:
                    t1, q1 = (t, q + 1) if q + 1 < QN else (t + 1, 0)
                    layer1(t1, q1)
                for k in range(GROUPS):
                    layer2(t, q, k)
                    if mlp_of is not None:
                        if k == 5:
                            mlp_h1(mlp_of)
                        if k == 8:
                            mlp_h2(mlp_of)
                        if k == 11:
                            mlp_y(mlp_of)

            turn_x(0)
            layer1(0, 0)
            step(0, 0)
            with pe.Fori(0, TILES - 1) as t:
                step(t, 1)
                turn_x(t + 1)
                step(t, 2)
                step(t, 3)
                step(t + 1, 0, mlp_of=t)
            step(TILES - 1, 1)
            step(TILES - 1, 2)
            step(TILES - 1, 3, ahead=False)
            mlp_h1(TILES - 1)
            mlp_h2(TILES - 1)
            mlp_y(TILES - 1)


_INS = (["dense_ctx", "ids"] + [f"tbl_{f}" for f in range(M)]
        + ["W_top1", "b_top1", "W_top2", "b_top2", "W_top3", "L0_rec_W1", "L0_rec_b1", "L0_rec_W2", "L0_rec_b2"])


def kernel(**inputs):
    import numpy as _np
    import concourse.bacc as _bacc
    from concourse.bass_utils import run_bass_kernel_spmd as _run

    nc = _bacc.Bacc("TRN2", target_bir_lowering=False, num_devices=1)
    arrays, args = {}, []
    for name in _INS:
        a = _np.ascontiguousarray(inputs[name])
        arrays[f"in_{name}_dram"] = a
        args.append(nc.dram_tensor(f"in_{name}_dram", a.shape, mybir.dt.from_np(a.dtype), kind="ExternalInput").ap())
    out = nc.dram_tensor("out_0_dram", (B, 1), F32, kind="ExternalOutput").ap()
    build(nc, args[0], args[1], args[2:2 + M], *args[2 + M:], out)
    r = _run(nc, [arrays], core_ids=[0])
    return r.results[0]["out_0_dram"]
```

```python
from contextlib import ExitStack

import concourse.bass as bass
from concourse import mybir

ALU = mybir.AluOpType
ACT = mybir.ActivationFunctionType
AX_X = mybir.AxisListType.X
F32 = mybir.dt.float32
F32R = mybir.dt.float32r
I32 = mybir.dt.int32

P = 128
B, M, D = 512, 39, 16
S = 128
TILES = B // P
QN = 4
DH = 2
DQ = D // QN
QH = QN // DH
N = DQ * P
CHUNKS = TILES * QN

SHIFTS = (M + 1) // 2 + 1
KG = P // M
L1_ROWS = KG * M
L1_TILES = SHIFTS // KG
X_ROWS = M + KG * L1_TILES - 1

MG = 4
HG = P // MG
J = M // MG
I = S // HG
SINGLE = M - MG * J
L2_TILES = I * J + SINGLE
XB = J + SINGLE
G3 = 3
JG = J // G3
GROUPS = L2_TILES // G3
G6 = 2
UNITS = -(-GROUPS // G6)
SPLIT_UNITS = [1, 3, 5]
WHOLE_UNITS = [u for u in range(UNITS) if u not in SPLIT_UNITS]
SPLIT = [k for k in range(GROUPS) if k // G6 in SPLIT_UNITS]
WHOLE = [k for k in range(GROUPS) if k // G6 not in SPLIT_UNITS]
RING = 2
WARM = 7
CUTS0, CUTS1 = (0, 3, 5, 7), (0, 3, 7)

H1, H2 = 512, 256
O1, O2 = H1 // P, H2 // P
DENSE = 16
SMALL = 6 + 2 * O2 + O1


def in_register(engine, value):
    return value if isinstance(value, int) else engine.snap(value)


def build(nc, dense_ctx, ids, tables, W_top1, b_top1, W_top2, b_top2, W_top3, W1, b1, W2, b2, out):
    assert SHIFTS == KG * L1_TILES and J % G3 == 0 and SINGLE == G3 and L2_TILES % G3 == 0
    assert I % G6 == 0 and GROUPS == G6 * (UNITS - 1) + 1
    assert UNITS == 7 and SPLIT_UNITS == [1, 3, 5]
    assert QN * len(WHOLE_UNITS) % RING == 0 and QN * len(SPLIT_UNITS) % RING == 0

    with ExitStack() as ctx:
        def sb(name, shape, dt=F32):
            return ctx.enter_context(nc.sbuf_tensor(name, shape, dt))

        def ps(name, shape):
            return ctx.enter_context(nc.psum_tensor(name, shape, F32))

        def sem(name):
            return ctx.enter_context(nc.semaphore(name))

        x_scratch = nc.dram_tensor("x_scratch", [CHUNKS, X_ROWS, N], F32)
        x1_scratch = nc.dram_tensor("x1_scratch", [2, S, N], F32)

        ident = sb("ident", [P, P])
        ids_sb = sb("ids_sb", [P, TILES, M], I32)
        dense_sb = sb("dense_sb", [P, TILES, DENSE])
        denseT = sb("denseT", [DENSE, TILES * P])
        emb = sb("emb", [P, M, D])
        xT = sb("xT", [DH * M, QN // DH, N])
        w1T = sb("w1T", [P, L1_TILES, S])
        w2T = sb("w2T", [P, len(WHOLE), G3, S])
        w2H = sb("w2H", [P, len(SPLIT), G3, S], F32R)
        w2L = sb("w2L", [P, len(SPLIT), G3, S], F32R)
        b1_sb = sb("b1_sb", [S, 1])
        b2_sb = sb("b2_sb", [S, 1])
        wt1a = sb("wt1a", [P, 2, H1])
        wt1b = sb("wt1b", [DENSE, H1])
        wt2 = sb("wt2", [P, O1, H2])
        wt3 = sb("wt3", [P, O2, 1])
        bt1 = sb("bt1", [P, O1])
        bt2 = sb("bt2", [P, O2])

        l1_a = sb("l1_a", [P, N])
        l1_b = sb("l1_b", [P, L1_TILES, N])
        x0_rep = sb("x0_rep", [P, XB, N])
        x1_rep = sb("x1_rep", [P, 2, I, N])
        whole = sb("whole", [P, RING, G6, G3, N])
        to_split = sb("to_split", [P, G6, G3, N])
        high = sb("high", [P, G6, G3, N], F32R)
        low = sb("low", [P, RING, G6, G3, N], F32R)
        x1 = sb("x1", [S, QN, DQ, P])
        x2 = sb("x2", [S, QN, DQ, P])
        p1 = sb("p1", [S, P])
        p2 = sb("p2", [S, 2, P])
        h1 = sb("h1", [P, O1, P])
        h2 = sb("h2", [P, O2, P])
        y_sb = sb("y_sb", [1, P])
        w2_raw = x0_rep[:].rearrange("p a n -> p (a n)")[:, 0:S * M].rearrange("p (h m) -> p h m", m=M)
        w2_packed = whole[:].rearrange("p a e c n -> p (a e c n)")[:, 0:I * J * P]
        w1_sym = x0_rep[:].rearrange("p a n -> p (a n)")[:, S * M:S * M + SHIFTS * M]
        w1_raw = x1_rep[:, 1, :, :].rearrange("p a n -> p (a n)")[:, 0:M * M]

        x1_ps = [ps(f"x1_ps{i}", [P, N]) for i in range(2)]
        x2_ps = [ps(f"x2_ps{i}", [P, N]) for i in range(2)]
        tr_ps = [ps(f"tr_ps{i}", [P, N]) for i in range(2)]
        h_ps = ps("h_ps", [P, N])
        y_ps = ps("y_ps", [P, N])
        last_h = [bank[:, 0:P] for bank in (h_ps, tr_ps[0], tr_ps[1], x1_ps[0])]

        ids_in = sem("ids_in")
        w1_in = sem("w1_in")
        w2_in = sem("w2_in")
        small_in = sem("small_in")
        ident_zero = sem("ident_zero")
        ident_ready = sem("ident_ready")
        gathered = sem("gathered")
        w1_symmetric = sem("w1_symmetric")
        w2_packed_act = sem("w2_packed_act")
        w2_packed_dve = sem("w2_packed_dve")
        w_turned = sem("w_turned")
        w_copied = sem("w_copied")
        w_low = sem("w_low")
        x_turned = sem("x_turned")
        x_copied = sem("x_copied")
        x_scratched = sem("x_scratched")
        l1_in = sem("l1_in")
        start_in = [[sem(f"start_in{g}_{part}") for part in range(len(cuts) - 1)]
                    for g, cuts in enumerate((CUTS0, CUTS1))]
        x0_rep_in = [sem(f"x0_rep_in{j}") for j in range(JG + 1)]
        x1_rep_in = [[sem(f"x1_rep_in{i}_{pair}") for pair in range(I // G6)] for i in range(2)]
        prod1_ready = sem("prod1_ready")
        l1_done = sem("l1_done")
        x1_ready = sem("x1_ready")
        x1_scratched = sem("x1_scratched")
        prod2_made = sem("prod2_made")
        high_ready = sem("high_ready")
        low_ready = sem("low_ready")
        whole_used = sem("whole_used")
        high_used = sem("high_used")
        low_used = sem("low_used")
        x2_ready = sem("x2_ready")
        p1_ready = sem("p1_ready")
        p2_ready = sem("p2_ready")
        h1_summed = sem("h1_summed")
        h1_ready = sem("h1_ready")
        h2_summed = sem("h2_summed")
        h2_ready = sem("h2_ready")
        y_summed = sem("y_summed")
        y_ready = sem("y_ready")
        y_out = sem("y_out")

        l1_parts = [(0, L1_TILES, l1_b[:], l1_in)]
        l1_parts0 = [(a, b, l1_b[:, a:b, :], arrived) for a, b, arrived in zip(CUTS0, CUTS0[1:], start_in[0])]
        l1_a1 = x2[:, 0, :, :].rearrange("s d b -> s (d b)")
        l1_b1 = (x2[:, 1:QN, :, :].rearrange("s q d b -> s q (d b)"),
                 whole[:, 1, :, :, :].rearrange("p e c n -> p (e c) n")[:, 0:CUTS1[2] - CUTS1[1], :])
        l1_parts1 = [(a, b, tiles, arrived) for a, b, tiles, arrived in zip(CUTS1, CUTS1[1:], l1_b1, start_in[1])]

        w1_tiles = [w1_sym[:, j * L1_ROWS:(j + 1) * L1_ROWS] for j in range(L1_TILES)]
        w2_tiles = [w2_packed[:, n * P:(n + 1) * P] for n in range(I * J)]
        w2_tiles += [w2_raw[:, :, J * MG + n] for n in range(SINGLE)]
        banks = [w1_tiles[0:3], w1_tiles[3:6], w1_tiles[6:7]]
        banks += [w2_tiles[n:n + G3] for n in range(0, L2_TILES, G3)]
        heights = [L1_ROWS] * 3 + [P] * GROUPS

        def pack_w2(engine_copy, k):
            g, i = divmod(k, I)
            dst = w2_packed[:, k * G3 * P:(k + 1) * G3 * P].rearrange("s (c h a) -> s c h a", c=G3, a=MG)
            src = w2_raw[:, i:S:I, 0:J * MG].rearrange("s h (a g c) -> s g c h a", a=MG, c=G3)[:, g]
            return engine_copy(dst, src)

        def bank_dst(n):
            if n < 3:
                return w1T[0:heights[n], 3 * n:3 * n + len(banks[n]), :]
            return w2H[:, SPLIT.index(n - 3)] if n - 3 in SPLIT else w2T[:, WHOLE.index(n - 3)]

        def bank_src(n):
            return tr_ps[n % 2][0:heights[n], 0:len(banks[n]) * S].rearrange("p (k s) -> p k s", s=S)

        BANKS = len(banks) + 1

        block = ctx.enter_context(nc.Block())

        @block.sync
        def _(sp):
            sp.dma_start(ids_sb[:], ids.rearrange("(t p) f -> p t f", p=P)).then_inc(ids_in, 16)
            sp.dma_start(w1_raw, W1.rearrange("s h m -> s (h m)")).then_inc(w1_in, 16)
            sp.dma_start(w2_raw, W2).then_inc(w2_in, 16)
            sp.dma_start(dense_sb[:], dense_ctx.rearrange("(t p) c -> p t c", p=P)).then_inc(small_in, 16)
            sp.dma_start(b1_sb[:], b1.rearrange("(s a) -> s a", a=1)).then_inc(small_in, 16)
            sp.dma_start(b2_sb[:], b2.rearrange("(s a) -> s a", a=1)).then_inc(small_in, 16)
            sp.dma_start(wt1a[:], W_top1[0:2 * P, :].rearrange("(k p) n -> p k n", p=P)).then_inc(small_in, 16)
            sp.dma_start(wt1b[:], W_top1[2 * P:2 * P + DENSE, :]).then_inc(small_in, 16)
            sp.dma_start(wt2[:], W_top2.rearrange("(k p) n -> p k n", p=P)).then_inc(small_in, 16)
            for vector, columns in ((W_top3.rearrange("k a -> (k a)"), wt3[:, :, 0]), (b_top1, bt1), (b_top2, bt2)):
                for k in range(vector.shape[0] // P):
                    sp.dma_start(columns[:, k:k + 1], vector[k * P:(k + 1) * P].rearrange("(p a) -> p a", a=1)
                                 ).then_inc(small_in, 16)

            def store_x_half(t, k, at):
                for base, rows in zip(at, (M, X_ROWS - M)):
                    dst = bass.AP(x_scratch, base + k * X_ROWS * N, [[N, rows], [QH * X_ROWS * N, DH], [1, N]])
                    sp.dma_start(dst, xT[0:DH * rows, k, :]).then_inc(x_scratched, 16)

            def store_x(t):
                at = [in_register(sp, (QN * t * X_ROWS + r0) * N) for r0 in (0, M)]
                sp.wait_ge(x_copied, QH * (t + 1))
                for k in range(QH):
                    store_x_half(t, k, at)

            def load_l1(t, q, factor=l1_a, parts=l1_parts):
                g = QN * t + q
                base = in_register(sp, g * X_ROWS * N)
                if q == 0 and not (isinstance(t, int) and t == 0):
                    sp.wait_ge(x_scratched, 16 * 2 * QH * (t + 1))
                sp.dma_start(factor[0:L1_ROWS, :],
                             bass.AP(x_scratch, base, [[N, M], [0, KG], [1, N]])).then_inc(parts[0][3], 16)
                for a, b, seconds, arrived in parts:
                    sp.dma_start(seconds[0:L1_ROWS, :, :],
                                 bass.AP(x_scratch, base + a * N, [[N, M], [L1_TILES * N, KG], [1, (b - a) * N]])
                                 ).then_inc(arrived, 16)

            def load_x0_rep(t, q, j):
                g = QN * t + q
                base = in_register(sp, g * X_ROWS * N)
                if not (isinstance(g, int) and g == 0):
                    used = UNITS * (g - 1) + (I // G6 * (j + 1) if j < JG else UNITS)
                    sp.wait_ge(prod2_made, used)
                if j < JG:
                    at, src = G3 * j * N, [[0, HG], [J * N, MG], [1, G3 * N]]
                else:
                    at, src = MG * J * N, [[0, P], [1, SINGLE * N]]
                sp.dma_start(x0_rep[:, G3 * j:G3 * (j + 1), :],
                             bass.AP(x_scratch, base + at, src)).then_inc(x0_rep_in[j], 16)

            def repeat_x1(t, q):
                g, par = QN * t + q, q % 2
                sp.wait_ge(x1_ready, g + 1)
                sp.dma_start(x1_scratch[par], x1[:, q, :, :].rearrange("s d b -> s (d b)")).then_inc(x1_scratched, 16)
                sp.wait_ge(x1_scratched, 16 * (g + 1))
                for pair in range(I // G6):
                    src = bass.AP(x1_scratch, (par * S + G6 * pair) * N, [[I * N, HG], [0, MG], [1, G6 * N]])
                    sp.dma_start(x1_rep[:, par, G6 * pair:G6 * (pair + 1), :], src
                                 ).then_inc(x1_rep_in[par][pair], 16)

            def step(t, q, ahead=True, ahead2=True, store_next=False):
                t1, q1 = (t, q + 1) if q + 1 < QN else (t + 1, 0)
                t2, q2 = (t, q + 2) if q + 2 < QN else (t + 1, q + 2 - QN)
                if ahead:
                    load_x0_rep(t1, q1, 0)
                    repeat_x1(t1, q1)
                    if ahead2:
                        load_l1(t2, q2)
                    for j in range(1, JG + 1):
                        load_x0_rep(t1, q1, j)
                if store_next:
                    store_x(t + 1)

            def store_y(t):
                at = in_register(sp, P * t)
                sp.wait_ge(y_ready, t + 1)
                sp.dma_start(bass.AP(out.tensor, at, [[P, 1], [1, P]]), y_sb[:]).then_inc(y_out, 16)

            sp.wait_ge(x_copied, 1)
            store_x_half(0, 0, (0, M * N))
            sp.wait_ge(x_scratched, 16 * 2)
            load_l1(0, 0, parts=l1_parts0)
            sp.wait_ge(x_copied, QH)
            store_x_half(0, 1, (0, M * N))
            sp.wait_ge(w_turned, BANKS)
            load_x0_rep(0, 0, 0)
            sp.wait_ge(x_scratched, 16 * 2 * QH)
            load_l1(0, 1, l1_a1, l1_parts1)
            repeat_x1(0, 0)
            for j in range(1, JG + 1):
                load_x0_rep(0, 0, j)
            step(0, 0)
            with sp.Fori(0, TILES - 1) as t:
                step(t, 1, store_next=True)
                step(t, 2)
                step(t, 3)
                step(t + 1, 0)
                store_y(t)
            step(TILES - 1, 1)
            step(TILES - 1, 2, ahead2=False)
            store_y(TILES - 1)
            sp.wait_ge(y_out, 16 * TILES)

        @block.gpsimd
        def _(pool):
            nc.gpsimd.memset(ident[:], 0.0).then_inc(ident_zero, 1)
            pool.wait_ge(ident_zero, 1)
            nc.gpsimd.affine_select(out=ident[:], in_=ident[:], compare_op=ALU.not_equal, fill=1.0, base=0,
                                    pattern=[[-1, P]], channel_multiplier=1).then_inc(ident_ready, 1)
            pool.wait_ge(ids_in, 16)
            for t in range(TILES):
                if t >= 1:
                    pool.wait_ge(x_turned, QH * t)
                for f in range(M):
                    nc.gpsimd.indirect_dma_start(
                        out=emb[:, f, :], out_offset=None, in_=tables[f],
                        in_offset=bass.IndirectOffsetOnAxis(ap=ids_sb[:, t, f:f + 1], axis=0)
                    ).then_inc(gathered, 16)

        @block.vector
        def _(dve):
            dve.wait_ge(w1_in, 16)

            def w1_run(first, count):
                return w1_raw[:, first:first + (count - 1) * (M + 1) + 1:M + 1]

            def w1_dst(k, h, count):
                at = k % L1_TILES * L1_ROWS + h * KG + k // L1_TILES
                return w1_sym[:, at:at + (count - 1) * KG + 1:KG]

            for k in range(SHIFTS):
                for h, m, count in ((0, k, M - k), (M - k, 0, k)):
                    if count == 0:
                        continue
                    if k in (0, SHIFTS - 2, SHIFTS - 1):
                        nc.vector.tensor_copy(w1_dst(k, h, count), w1_run(h * M + m, count)
                                              ).then_inc(w1_symmetric, 1)
                    else:
                        nc.vector.tensor_tensor(w1_dst(k, h, count), w1_run(h * M + m, count),
                                                w1_run(m * M + h, count), ALU.add).then_inc(w1_symmetric, 1)
            dve.wait_ge(w2_in, 16)
            for k in range(I * JG // 2, I * JG):
                pack_w2(nc.vector.tensor_copy, k).then_inc(w2_packed_dve, 1)
            for b, k in enumerate(SPLIT):
                dve.wait_ge(w_copied, k + 3 + 1)
                nc.vector.tensor_tensor(w2L[:, b], bank_src(k + 3), w2H[:, b].bitcast(F32),
                                        ALU.subtract).then_inc(w_low, 1)

            def products1(t, q, factor=l1_a, parts=l1_parts):
                g = QN * t + q
                for a, b, seconds, arrived in parts:
                    if parts is l1_parts:
                        dve.wait_ge(arrived, 16 * 2 * (g - 1))
                    else:
                        dve.wait_ge(arrived, 16 * (2 if a == 0 else 1))
                    nc.vector.tensor_tensor(
                        seconds[0:L1_ROWS, :, :], factor[0:L1_ROWS, None, :].to_broadcast([L1_ROWS, b - a, N]),
                        seconds[0:L1_ROWS, :, :], ALU.mult).then_inc(prod1_ready, 1)

            def product2(t, q, u):
                g, par = QN * t + q, q % 2
                j, pair = divmod(u, I // G6)
                if u < I // G6:
                    dve.wait_ge(x1_rep_in[par][u], 16 * (2 * t + q // 2 + 1))
                if pair == 0:
                    dve.wait_ge(x0_rep_in[j], 16 * (g + 1))
                if u in WHOLE_UNITS:
                    n = len(WHOLE_UNITS) * g + WHOLE_UNITS.index(u)
                    dst = whole[:, (len(WHOLE_UNITS) * q + WHOLE_UNITS.index(u)) % RING]
                    if not (isinstance(n, int) and n < RING):
                        dve.wait_ge(whole_used, n - RING + 1)
                else:
                    n = len(SPLIT_UNITS) * g + SPLIT_UNITS.index(u)
                    dst = to_split[:]
                    if not (isinstance(n, int) and n == 0):
                        dve.wait_ge(low_ready, n)
                x0_rows = x0_rep[:, None, G3 * j:G3 * (j + 1), :]
                if j < JG:
                    a = x1_rep[:, par, G6 * pair:G6 * (pair + 1), None, :].to_broadcast([P, G6, G3, N])
                    x0_rows = x0_rows.to_broadcast([P, G6, G3, N])
                else:
                    dst = dst[:, 0:1]
                    a = x1[:, q, :, :].rearrange("s d b -> s (d b)")[:, None, None, :].to_broadcast([P, 1, G3, N])
                nc.vector.tensor_tensor(dst, a, x0_rows, ALU.mult).then_inc(prod2_made, 1)

            def low_part(t, q, u):
                b = SPLIT_UNITS.index(u)
                n = len(SPLIT_UNITS) * (QN * t + q) + b
                slot = (len(SPLIT_UNITS) * q + b) % RING
                if not (isinstance(n, int) and n < RING):
                    dve.wait_ge(low_used, n - RING + 1)
                dve.wait_ge(high_ready, n + 1)
                nc.vector.tensor_tensor(low[:, slot], to_split[:], high[:].bitcast(F32),
                                        ALU.subtract).then_inc(low_ready, 1)

            def sum_d(dst, x, done):
                nc.vector.tensor_reduce(dst, x.rearrange("s q d b -> s b (q d)"), AX_X, ALU.add).then_inc(done, 1)

            def step(t, q, layer1_ahead=True, last=False, sum_x2_of=None):
                t1, q1 = (t, q + 1) if q + 1 < QN else (t + 1, 0)
                product2(t, q, 1)
                if layer1_ahead:
                    products1(t1, q1)
                    low_part(t, q, 1)
                    product2(t, q, 2)
                else:
                    product2(t, q, 2)
                    low_part(t, q, 1)
                if sum_x2_of is not None:
                    dve.wait_ge(x2_ready, QN * (sum_x2_of + 1))
                    sum_d(p2[:, 0, :], x2[:], p2_ready)
                product2(t, q, 3)
                product2(t, q, 4)
                low_part(t, q, 3)
                product2(t, q, 5)
                product2(t, q, 6)
                if q == 2:
                    dve.wait_ge(x1_ready, QN * (t + 1))
                    sum_d(p1[:], x1[:], p1_ready)
                if last:
                    dve.wait_ge(x2_ready, CHUNKS - 1)
                    sum_d(p2[:, 0, :], x2[:, 0:QN - 1], p2_ready)
                else:
                    product2(t1, q1, 0)
                low_part(t, q, 5)

            products1(0, 0, parts=l1_parts0)
            products1(0, 1, l1_a1, l1_parts1)
            product2(0, 0, 0)
            dve.wait_ge(l1_done, 2)
            step(0, 0, layer1_ahead=False)
            with dve.Fori(0, TILES - 1) as t:
                step(t, 1)
                step(t, 2)
                step(t, 3)
                step(t + 1, 0, sum_x2_of=t)
            step(TILES - 1, 1)
            step(TILES - 1, 2)
            step(TILES - 1, 3, layer1_ahead=False, last=True)
            dve.wait_ge(x2_ready, CHUNKS)
            sum_d(p2[:, 1, :], x2[:, 3:4], p2_ready)

        @block.scalar
        def _(act):
            act.wait_ge(w2_in, 16)
            for k in range(I * JG // 2):
                pack_w2(nc.scalar.copy, k).then_inc(w2_packed_act, 1)
            for n in range(len(banks)):
                act.wait_ge(w_turned, n + 1)
                nc.scalar.copy(bank_dst(n), bank_src(n)).then_inc(w_copied, 1)
            act.wait_ge(w_turned, BANKS)
            nc.scalar.copy(denseT[:], tr_ps[(BANKS - 1) % 2][0:DENSE, 0:TILES * P]).then_inc(w_copied, 1)
            act.wait_ge(small_in, 16 * SMALL)

            def copy_x(t):
                for k in range(QH):
                    act.wait_ge(x_turned, QH * t + k + 1)
                    if k == 0 and not (isinstance(t, int) and t == 0):
                        act.wait_ge(x_scratched, 16 * 2 * QH * t)
                    nc.scalar.copy(xT[:, k, :], tr_ps[k % 2][0:DH * M, :]).then_inc(x_copied, 1)

            def finish_x1(t, q):
                act.wait_ge(l1_done, QN * t + q + 1)
                nc.scalar.activation(x1[:, q, :, :].rearrange("s d b -> s (d b)"), x1_ps[q % 2][:], ACT.Relu,
                                     bias=b1_sb[:, 0:1]).then_inc(x1_ready, 1)

            def finish_x2(t, q):
                act.wait_ge(low_used, len(SPLIT_UNITS) * (QN * t + q + 1))
                nc.scalar.activation(x2[:, q, :, :].rearrange("s d b -> s (d b)"), x2_ps[q % 2][:], ACT.Relu,
                                     bias=b2_sb[:, 0:1]).then_inc(x2_ready, 1)

            def high_part(t, q, u):
                b = SPLIT_UNITS.index(u)
                n = len(SPLIT_UNITS) * (QN * t + q) + b
                if not (isinstance(n, int) and n == 0):
                    act.wait_ge(high_used, n)
                act.wait_ge(prod2_made, UNITS * (QN * t + q) + u + 1)
                nc.scalar.copy(high[:], to_split[:]).then_inc(high_ready, 1)

            def mlp_h1(t):
                act.wait_ge(h1_summed, t + 1)
                for o in range(O1):
                    nc.scalar.activation(h1[:, o, :], h_ps[:, o * P:(o + 1) * P], ACT.Relu,
                                         bias=bt1[:, o:o + 1]).then_inc(h1_ready, 1)

            def mlp_h2(t):
                act.wait_ge(h2_summed, t + 1)
                for o in range(O2):
                    nc.scalar.activation(h2[:, o, :], h_ps[:, o * P:(o + 1) * P], ACT.Relu,
                                         bias=bt2[:, o:o + 1]).then_inc(h2_ready, 1)

            def mlp_y(t):
                act.wait_ge(y_summed, t + 1)
                if not (isinstance(t, int) and t == 0):
                    act.wait_ge(y_out, 16 * t)
                nc.scalar.copy(y_sb[:], y_ps[0:1, 0:P]).then_inc(y_ready, 1)

            def step(t, q, layer1_ahead=True, copy_next=False, mlp_of=None):
                for u in SPLIT_UNITS:
                    high_part(t, q, u)
                    if u == 1:
                        if q > 0:
                            finish_x2(t, q - 1)
                        elif not isinstance(t, int):
                            finish_x2(t - 1, QN - 1)
                        if layer1_ahead:
                            t1, q1 = (t, q + 1) if q + 1 < QN else (t + 1, 0)
                            finish_x1(t1, q1)
                    if u == 3 and mlp_of is not None:
                        mlp_h1(mlp_of)
                    if u == 5 and mlp_of is not None:
                        mlp_h2(mlp_of)
                        mlp_y(mlp_of)
                if copy_next:
                    copy_x(t + 1)

            copy_x(0)
            finish_x1(0, 0)
            finish_x1(0, 1)
            step(0, 0, layer1_ahead=False)
            with act.Fori(0, TILES - 1) as t:
                step(t, 1, copy_next=True)
                step(t, 2)
                step(t, 3)
                step(t + 1, 0, mlp_of=t)
            step(TILES - 1, 1)
            step(TILES - 1, 2)
            step(TILES - 1, 3, layer1_ahead=False)
            finish_x2(TILES - 1, QN - 1)
            for o in range(O1):
                act.wait_ge(h1_summed, TILES - 1 + o + 1)
                nc.scalar.activation(h1[:, o, :], last_h[o], ACT.Relu, bias=bt1[:, o:o + 1]).then_inc(h1_ready, 1)
            act.wait_ge(h2_summed, TILES)
            for o in range(O2):
                nc.scalar.activation(h2[:, o, :], x2_ps[o][:, 0:P], ACT.Relu, bias=bt2[:, o:o + 1]
                                     ).then_inc(h2_ready, 1)
            mlp_y(TILES - 1)

        @block.tensor
        def _(pe):
            pe.wait_ge(ident_ready, 1)

            def copied(n):
                pe.wait_ge(w_copied, n + 1)
                if n - 3 in SPLIT:
                    pe.wait_ge(w_low, SPLIT.index(n - 3) + 1)

            for n, bank in enumerate(banks):
                if n == 0:
                    pe.wait_ge(w1_symmetric, 2 * SHIFTS - 1)
                if n == 3:
                    pe.wait_ge(w2_packed_act, I * JG // 2)
                    pe.wait_ge(w2_packed_dve, I * JG - I * JG // 2)
                if n >= 2:
                    copied(n - 2)
                for k, src in enumerate(bank):
                    last = nc.tensor.transpose(tr_ps[n % 2][0:heights[n], k * S:(k + 1) * S], src, ident[:])
                last.then_inc(w_turned, 1)
            pe.wait_ge(small_in, 16 * SMALL)
            copied(BANKS - 3)
            for t in range(TILES):
                last = nc.tensor.transpose(tr_ps[(BANKS - 1) % 2][0:DENSE, t * P:(t + 1) * P], dense_sb[:, t, :],
                                           ident[:])
            last.then_inc(w_turned, 1)
            copied(BANKS - 2)
            copied(BANKS - 1)

            def turn_x(t):
                pe.wait_ge(gathered, 16 * M * (t + 1))
                for k in range(QH):
                    for d in range(DQ):
                        src = emb[:].rearrange("b f (e d) -> b (f e) d", e=DH)[:, :, k * DQ + d]
                        last = nc.tensor.transpose(tr_ps[k][0:DH * M, d * P:(d + 1) * P], src, ident[:])
                    last.then_inc(x_turned, 1)

            def layer1(t, q, parts=l1_parts):
                g = QN * t + q
                if not (isinstance(g, int) and g < 2):
                    pe.wait_ge(x1_ready, g - 1)
                for n, (a, b, products, _) in enumerate(parts):
                    parts_before = len(l1_parts0) + len(l1_parts1) + g - 2 if parts is l1_parts else \
                        len(l1_parts0) * g
                    pe.wait_ge(prod1_ready, parts_before + n + 1)
                    for j in range(a, b):
                        last = nc.tensor.matmul(x1_ps[q % 2][:], w1T[0:L1_ROWS, j, :],
                                                products[0:L1_ROWS, j - a, :],
                                                start=(j == 0), stop=(j == L1_TILES - 1))
                last.then_inc(l1_done, 1)

            def tiles_of(u):
                return [(k, k - G6 * u, c) for k in range(G6 * u, min(G6 * (u + 1), GROUPS)) for c in range(G3)]

            def whole_unit(t, q, u):
                g = QN * t + q
                a = WHOLE_UNITS.index(u)
                slot = (len(WHOLE_UNITS) * q + a) % RING
                if u == 0 and not (isinstance(g, int) and g < 2):
                    pe.wait_ge(x2_ready, g - 1)
                pe.wait_ge(prod2_made, UNITS * g + u + 1)
                for k, e, c in tiles_of(u):
                    last = nc.tensor.matmul(x2_ps[q % 2][:], w2T[:, WHOLE.index(k), c, :], whole[:, slot, e, c, :],
                                            start=(k == 0 and c == 0), stop=False)
                last.then_inc(whole_used, 1)

            def high_unit(t, q, u):
                b = SPLIT_UNITS.index(u)
                pe.wait_ge(high_ready, len(SPLIT_UNITS) * (QN * t + q) + b + 1)
                for k, e, c in tiles_of(u):
                    for w in (w2L, w2H):
                        last = nc.tensor.matmul(x2_ps[q % 2][:], w[:, SPLIT.index(k), c, :], high[:, e, c, :],
                                                start=False, stop=False)
                last.then_inc(high_used, 1)

            def low_unit(t, q, u):
                b = SPLIT_UNITS.index(u)
                slot = (len(SPLIT_UNITS) * q + b) % RING
                pe.wait_ge(low_ready, len(SPLIT_UNITS) * (QN * t + q) + b + 1)
                for k, e, c in tiles_of(u):
                    last = nc.tensor.matmul(x2_ps[q % 2][:], w2H[:, SPLIT.index(k), c, :], low[:, slot, e, c, :],
                                            start=False, stop=(k == SPLIT[-1] and c == G3 - 1))
                last.then_inc(low_used, 1)

            def mlp_h1(t):
                pe.wait_ge(p1_ready, t + 1)
                pe.wait_ge(p2_ready, t + 1)
                for o in range(O1):
                    cols = slice(o * P, (o + 1) * P)
                    nc.tensor.matmul(h_ps[:, cols], wt1a[:, 0, cols], p1[:], start=True, stop=False)
                    nc.tensor.matmul(h_ps[:, cols], wt1a[:, 1, cols], p2[:, 0, :], start=False, stop=False)
                    last = nc.tensor.matmul(h_ps[:, cols], wt1b[:, cols], denseT[:, bass.ts(t, P)],
                                            start=False, stop=True)
                last.then_inc(h1_summed, 1)

            def last_mlp_h1():
                t = TILES - 1
                pe.wait_ge(p1_ready, t + 1)
                pe.wait_ge(p2_ready, t + 1)
                for o in range(O1):
                    cols = slice(o * P, (o + 1) * P)
                    nc.tensor.matmul(last_h[o], wt1a[:, 0, cols], p1[:], start=True, stop=False)
                    nc.tensor.matmul(last_h[o], wt1a[:, 1, cols], p2[:, 0, :], start=False, stop=False)
                    nc.tensor.matmul(last_h[o], wt1b[:, cols], denseT[:, t * P:(t + 1) * P], start=False, stop=False)
                pe.wait_ge(p2_ready, t + 2)
                for o in range(O1):
                    nc.tensor.matmul(last_h[o], wt1a[:, 1, o * P:(o + 1) * P], p2[:, 1, :],
                                     start=False, stop=True).then_inc(h1_summed, 1)

            def mlp_h2(t):
                pe.wait_ge(h1_ready, O1 * (t + 1))
                for o in range(O2):
                    cols = slice(o * P, (o + 1) * P)
                    for k in range(O1):
                        last = nc.tensor.matmul(h_ps[:, cols], wt2[:, k, cols], h1[:, k, :],
                                                start=(k == 0), stop=(k == O1 - 1))
                last.then_inc(h2_summed, 1)

            def last_mlp_h2():
                for k in range(O1):
                    pe.wait_ge(h1_ready, O1 * (TILES - 1) + k + 1)
                    for o in range(O2):
                        last = nc.tensor.matmul(x2_ps[o][:, 0:P], wt2[:, k, o * P:(o + 1) * P], h1[:, k, :],
                                                start=(k == 0), stop=(k == O1 - 1))
                last.then_inc(h2_summed, 1)

            def mlp_y(t):
                pe.wait_ge(h2_ready, O2 * (t + 1))
                for k in range(O2):
                    last = nc.tensor.matmul(y_ps[0:1, 0:P], wt3[:, k, :], h2[:, k, :],
                                            start=(k == 0), stop=(k == O2 - 1))
                last.then_inc(y_summed, 1)

            def step(t, q, layer1_ahead=True, last=False, turn_next=False, mlp_of=None):
                t1, q1 = (t, q + 1) if q + 1 < QN else (t + 1, 0)
                high_unit(t, q, 1)
                if layer1_ahead:
                    layer1(t1, q1)
                    low_unit(t, q, 1)
                    whole_unit(t, q, 2)
                else:
                    whole_unit(t, q, 2)
                    low_unit(t, q, 1)
                if mlp_of is not None:
                    mlp_h1(mlp_of)
                high_unit(t, q, 3)
                whole_unit(t, q, 4)
                low_unit(t, q, 3)
                if turn_next:
                    turn_x(t + 1)
                if mlp_of is not None:
                    mlp_h2(mlp_of)
                high_unit(t, q, 5)
                whole_unit(t, q, 6)
                if mlp_of is not None:
                    mlp_y(mlp_of)
                if not last:
                    whole_unit(t1, q1, 0)
                low_unit(t, q, 5)

            def keep_warm(count):
                for _ in range(count):
                    nc.tensor.matmul(h_ps[:], ident[:], wt1a[:, 0, :], start=True, stop=True)

            turn_x(0)
            keep_warm(WARM)
            layer1(0, 0, l1_parts0)
            layer1(0, 1, l1_parts1)
            whole_unit(0, 0, 0)
            step(0, 0, layer1_ahead=False)
            with pe.Fori(0, TILES - 1) as t:
                step(t, 1, turn_next=True)
                step(t, 2)
                step(t, 3)
                step(t + 1, 0, mlp_of=t)
            step(TILES - 1, 1)
            step(TILES - 1, 2)
            step(TILES - 1, 3, layer1_ahead=False, last=True)
            last_mlp_h1()
            last_mlp_h2()
            mlp_y(TILES - 1)


_INS = (["dense_ctx", "ids"] + [f"tbl_{f}" for f in range(M)]
        + ["W_top1", "b_top1", "W_top2", "b_top2", "W_top3", "L0_rec_W1", "L0_rec_b1", "L0_rec_W2", "L0_rec_b2"])


def kernel(**inputs):
    import numpy as _np
    import concourse.bacc as _bacc
    from concourse.bass_utils import run_bass_kernel_spmd as _run

    nc = _bacc.Bacc("TRN2", target_bir_lowering=False, num_devices=1)
    arrays, args = {}, []
    for name in _INS:
        a = _np.ascontiguousarray(inputs[name])
        arrays[f"in_{name}_dram"] = a
        args.append(nc.dram_tensor(f"in_{name}_dram", a.shape, mybir.dt.from_np(a.dtype), kind="ExternalInput").ap())
    out = nc.dram_tensor("out_0_dram", (B, 1), F32, kind="ExternalOutput").ap()
    build(nc, args[0], args[1], args[2:2 + M], *args[2 + M:], out)
    r = _run(nc, [arrays], core_ids=[0])
    return r.results[0]["out_0_dram"]
```
